# Optimizing a Trainium2 kernel written in Bass

```python
import numpy as np
import jax
import jax.numpy as jnp

def _softmax(x, axis=-1):
    return jax.nn.softmax(x, axis=axis)

def _gelu(x):
    return jax.nn.gelu(x, approximate=True)

def _silu(x):
    return jax.nn.silu(x)

def _sigmoid(x):
    return jax.nn.sigmoid(x)

def _layernorm(x, axis=-1, eps=1e-05):
    m = jnp.mean(x, axis=axis, keepdims=True)
    v = jnp.var(x, axis=axis, keepdims=True)
    return (x - m) / jnp.sqrt(v + eps)

def _scatter_add(tgt, idx, src, axis=0):
    return tgt.at[idx].add(src)

def _segment_sum(src, seg, n):
    return jax.ops.segment_sum(src, seg, n)
kernel_name = 'mk_cond_seq_d2_seqx_r2_afaad2'

def setup_inputs(seed: int=0):
    np.random.seed(seed)
    _w = jnp.asarray

    def _rec_inputs():
        import jax
        import jax.numpy as jnp
        _rk = jax.random.key(seed)
        x = 0.4999 + 0.2886 * jax.random.normal(jax.random.fold_in(_rk, 1), (32, 512, 512), jnp.float32)
        _lenS = 512 - jax.random.randint(jax.random.fold_in(_rk, 7), (32,), 0, max(1, 512 // 4) + 1, jnp.int32)
        _lenS2 = 512 - jax.random.randint(jax.random.fold_in(_rk, 8), (32,), 0, max(1, 512 // 4) + 1, jnp.int32)
        condB_dt = jax.random.uniform(jax.random.fold_in(_rk, 11), (32,), jnp.float32, 0.0, 0.981965)
        itok_B_0_15 = jax.random.randint(jax.random.fold_in(_rk, 12), (32,), 0, 16, jnp.int32)
        return (x, condB_dt, itok_B_0_15)
    x, condB_dt, itok_B_0_15 = _rec_inputs()

    def _L0_cond_setup():
        import jax, jax.numpy as jnp
        import numpy as np
        B, NX, NY = (16, 512, 512)

        def _grad(f, axis):
            fm = jnp.moveaxis(f, axis, -1)
            g = (jnp.roll(fm, -1, -1) - jnp.roll(fm, 1, -1)) * 0.5
            g0 = (-3.0 * fm[..., 0] + 4.0 * fm[..., 1] - fm[..., 2]) * 0.5
            gN = (3.0 * fm[..., -1] - 4.0 * fm[..., -2] + fm[..., -3]) * 0.5
            g = g.at[..., 0].set(g0).at[..., -1].set(gN)
            return jnp.moveaxis(g, -1, axis)

        def _grad2(f, axis):
            fm = jnp.moveaxis(f, axis, -1)
            g = jnp.roll(fm, -1, -1) - 2.0 * fm + jnp.roll(fm, 1, -1)
            g0 = 2.0 * fm[..., 0] - 5.0 * fm[..., 1] + 4.0 * fm[..., 2] - fm[..., 3]
            gN = 2.0 * fm[..., -1] - 5.0 * fm[..., -2] + 4.0 * fm[..., -3] - fm[..., -4]
            g = g.at[..., 0].set(g0).at[..., -1].set(gN)
            return jnp.moveaxis(g, -1, axis)
        key = jax.random.key(seed)
        k1, k2, k3, k4 = jax.random.split(key, 4)
        f = jax.random.uniform(k1, (B, NX, NY), dtype=jnp.float32)
        A_grid = jax.random.normal(k2, (2, NX, NY), dtype=jnp.float32)
        B_grid = jax.random.uniform(k3, (3, NX, NY), dtype=jnp.float32)
        dt = jax.random.uniform(k4, (B,), dtype=jnp.float32)
        return {'f': f, 'A_grid': A_grid, 'B_grid': B_grid, 'dt': dt}
    _L0_cond_all = _L0_cond_setup()
    _L0_cond_in = {k: v for k, v in _L0_cond_all.items() if k in ('A_grid', 'B_grid')}
    del _L0_cond_all

    def _L1_cond_setup():
        import jax, jax.numpy as jnp
        import numpy as np
        B, S, D = (32, 512, 512)
        A = 128
        E = 16
        LN_EPS = 1e-05
        key = jax.random.key(seed)
        ks = jax.random.split(key, 10)
        s = lambda fan_in: 1.0 / np.sqrt(fan_in)
        return {'hidden_states': jax.random.normal(ks[0], (B, S, D), dtype=jnp.float32), 'domain_id': jax.random.randint(ks[1], (B,), 0, E, dtype=jnp.int64), 'down_W': jax.random.uniform(ks[2], (A, D), jnp.float32, -s(D), s(D)), 'down_b': jax.random.uniform(ks[3], (A,), jnp.float32, -s(D), s(D)), 'up_W': jax.random.uniform(ks[4], (D, A), jnp.float32, -s(A), s(A)), 'up_b': jax.random.uniform(ks[5], (D,), jnp.float32, -s(A), s(A)), 'expert_W': jax.random.uniform(ks[6], (E, A, A), jnp.float32, -s(A), s(A)), 'expert_b': jax.random.uniform(ks[7], (E, A), jnp.float32, -s(A), s(A)), 'domain_emb': jax.random.normal(ks[8], (E, A), dtype=jnp.float32), 'ln_gamma': jnp.ones((D,), jnp.float32), 'ln_beta': jnp.zeros((D,), jnp.float32)}
    _L1_cond_all = _L1_cond_setup()
    _L1_cond_in = {k: v for k, v in _L1_cond_all.items() if k in ('down_W', 'down_b', 'up_W', 'up_b', 'expert_W', 'expert_b', 'domain_emb', 'ln_gamma', 'ln_beta')}
    del _L1_cond_all
    return {'x': x, 'condB_dt': condB_dt, 'itok_B_0_15': itok_B_0_15, 'L0_cond_A_grid': _L0_cond_in['A_grid'], 'L0_cond_B_grid': _L0_cond_in['B_grid'], 'L1_cond_down_W': _L1_cond_in['down_W'], 'L1_cond_down_b': _L1_cond_in['down_b'], 'L1_cond_up_W': _L1_cond_in['up_W'], 'L1_cond_up_b': _L1_cond_in['up_b'], 'L1_cond_expert_W': _L1_cond_in['expert_W'], 'L1_cond_expert_b': _L1_cond_in['expert_b'], 'L1_cond_domain_emb': _L1_cond_in['domain_emb'], 'L1_cond_ln_gamma': _L1_cond_in['ln_gamma'], 'L1_cond_ln_beta': _L1_cond_in['ln_beta']}

def reference(x, condB_dt, itok_B_0_15, L0_cond_A_grid, L0_cond_B_grid, L1_cond_down_W, L1_cond_down_b, L1_cond_up_W, L1_cond_up_b, L1_cond_expert_W, L1_cond_expert_b, L1_cond_domain_emb, L1_cond_ln_gamma, L1_cond_ln_beta):
    import jax
    import jax.numpy as jnp

    def _L0_cond_ref(f, A_grid, B_grid, dt):
        import jax, jax.numpy as jnp
        import numpy as np
        B, NX, NY = (16, 512, 512)

        def _grad(f, axis):
            fm = jnp.moveaxis(f, axis, -1)
            g = (jnp.roll(fm, -1, -1) - jnp.roll(fm, 1, -1)) * 0.5
            g0 = (-3.0 * fm[..., 0] + 4.0 * fm[..., 1] - fm[..., 2]) * 0.5
            gN = (3.0 * fm[..., -1] - 4.0 * fm[..., -2] + fm[..., -3]) * 0.5
            g = g.at[..., 0].set(g0).at[..., -1].set(gN)
            return jnp.moveaxis(g, -1, axis)

        def _grad2(f, axis):
            fm = jnp.moveaxis(f, axis, -1)
            g = jnp.roll(fm, -1, -1) - 2.0 * fm + jnp.roll(fm, 1, -1)
            g0 = 2.0 * fm[..., 0] - 5.0 * fm[..., 1] + 4.0 * fm[..., 2] - fm[..., 3]
            gN = 2.0 * fm[..., -1] - 5.0 * fm[..., -2] + 4.0 * fm[..., -3] - fm[..., -4]
            g = g.at[..., 0].set(g0).at[..., -1].set(gN)
            return jnp.moveaxis(g, -1, axis)
        Af = A_grid[None] * f[:, None]
        Bf = B_grid[None] * f[:, None]
        gradv_Af = _grad(Af[:, 0], 1) + _grad(Af[:, 1], 2)
        gradvv_Bf = _grad2(Bf[:, 0], 1) + _grad2(Bf[:, 1], 2) + _grad(_grad(Bf[:, 2], 2), 1) + _grad(_grad(Bf[:, 2], 1), 2)
        df = -gradv_Af + gradvv_Bf * 0.5
        f_new = f + df * dt[:, None, None]
        return jnp.maximum(f_new, 0.0)

    def _L1_cond_ref(hidden_states, domain_id, down_W, down_b, up_W, up_b, expert_W, expert_b, domain_emb, ln_gamma, ln_beta):
        import jax, jax.numpy as jnp
        import numpy as np
        B, S, D = (32, 512, 512)
        A = 128
        E = 16
        LN_EPS = 1e-05
        residual = hidden_states
        hidden = jnp.einsum('bsd,ad->bsa', hidden_states, down_W) + down_b
        hidden = jax.nn.gelu(hidden, approximate=False)
        valid = (domain_id >= 0) & (domain_id < E)
        idx = jnp.clip(domain_id, 0, E - 1)
        Wsel = expert_W[idx]
        bsel = expert_b[idx]
        expert_out = jnp.einsum('bsa,boa->bso', hidden, Wsel) + bsel[:, None, :]
        domain_output = jnp.where(valid[:, None, None], expert_out, hidden)
        hidden = domain_output + domain_emb[idx][:, None, :]
        hidden = jnp.einsum('bsa,da->bsd', hidden, up_W) + up_b
        x = hidden + residual
        mu = jnp.mean(x, axis=-1, keepdims=True)
        var = jnp.mean(jnp.square(x - mu), axis=-1, keepdims=True)
        return (x - mu) * jax.lax.rsqrt(var + LN_EPS) * ln_gamma + ln_beta
    x = _L0_cond_ref(x, L0_cond_A_grid, L0_cond_B_grid, condB_dt)
    x = _L1_cond_ref(x, itok_B_0_15, L1_cond_down_W, L1_cond_down_b, L1_cond_up_W, L1_cond_up_b, L1_cond_expert_W, L1_cond_expert_b, L1_cond_domain_emb, L1_cond_ln_gamma, L1_cond_ln_beta)
    return x

_drawn_inputs = setup_inputs


def setup_inputs(seed=0):
    import zlib

    import numpy as np

    out = dict(_drawn_inputs(seed))
    spreads = {'L1_cond_ln_gamma': (1.0, 0.2), 'L1_cond_ln_beta': (0.0, 0.1)}
    factors = {'L1_cond_down_b': 8.0}
    for name, (base, spread) in spreads.items():
        noise = np.random.default_rng([zlib.crc32(name.encode()), seed]).standard_normal(out[name].shape)
        drawn = base * np.exp(spread * noise) if base else spread * noise
        out[name] = jnp.asarray(drawn.astype(out[name].dtype))
    for name, factor in factors.items():
        out[name] = (out[name] * factor).astype(out[name].dtype)
    return out
```

```python
import concourse.bass as bass
from concourse import mybir
from contextlib import ExitStack


def stencil_adapter_kernel(nc, x, dt_b, expert_id, A_grid, B_grid, down_W, down_b, up_W, up_b,
                           expert_W, expert_b, domain_emb, ln_gamma, ln_beta, out):
    fp32, i32 = mybir.dt.float32, mybir.dt.int32
    ALU, ACT, AX = mybir.AluOpType, mybir.ActivationFunctionType, mybir.AxisListType

    NB, S, DD = x.shape
    A, E = down_b.shape[0], expert_b.shape[0]
    P = 128
    T = S // P
    CB = DD // P
    H = DD // 2
    EPS = 1e-5
    KEEP0, KEEPN, ROWS = E, E + 1, E + 2
    V_UPB, V_DOWNB = ROWS, ROWS + CB
    GRAD = (3.0, -3.0, 1.0, 0.0)
    GRAD2 = (4.0, -6.0, 4.0, -1.0)
    EDGE = (-3.0, 4.0, -1.0)

    x_v = x.rearrange("b (p t) d -> b p (t d)", t=T)
    out_v = out.rearrange("b (p t) d -> b p (t d)", t=T)
    grid_v = [g.rearrange("c (p t) d -> c p t d", t=T) for g in (A_grid, B_grid)]
    comb_dram = nc.dram_tensor("comb_dram", [ROWS, P, DD + CB], fp32, kind="Internal").ap()

    ctx = ExitStack()
    with ctx:
        def sb(name, shape, dt=fp32):
            return ctx.enter_context(nc.sbuf_tensor(name, shape, dt))

        def pb(name, shape):
            return ctx.enter_context(nc.psum_tensor(name, shape, fp32))

        def sem(name):
            return ctx.enter_context(nc.semaphore(name))

        c_xp, c_xm, c_yp, c_ym, c_c, c_z = (sb(n, [P, T, DD]) for n in ("c_xp", "c_xm", "c_yp", "c_ym", "c_c", "c_z"))
        c_yghost = sb("c_yghost", [P, 2, T, 4])
        c_dedge = sb("c_dedge", [P, 2, T, 3])
        wide = sb("wide", [P, P + 4])
        ident, shift_up, shift_down = wide[:, 2:P + 2], wide[:, 3:P + 3], wide[:, 1:P + 1]
        dts = sb("dts", [P, NB])
        gamma, beta = sb("gamma", [P, DD]), sb("beta", [P, DD])
        downT = sb("downT", [P, CB, A])
        upT = sb("upT", [A, DD])
        vecT = sb("vecT", [P, P])
        biasT = sb("biasT", [P, CB, ROWS])
        rows = sb("rows", [1, NB], i32)
        ghosts = sb("ghosts", [P, DD])
        minus_half, one_over_d, eps = (sb(n, [P, 2]) for n in ("minus_half", "one_over_d", "eps"))
        f = sb("f", [P, 2, T, DD])
        u = sb("u", [P, 2, T, DD])
        U, V, Yp, Ym, C = (sb(n, [P, 2, T, H]) for n in ("U", "V", "Yp", "Ym", "C"))
        Z = sb("Z", [P, T, DD])
        D = sb("D", [P, T, H])
        yg_part = sb("yg_part", [P, 2, T, 4])
        de_part = sb("de_part", [P, 2, T, 3])
        xT = sb("xT", [P, CB, S])
        xbT = sb("xbT", [P, CB, S])
        hT = sb("hT", [A, S])
        comb = sb("comb", [P, 2, DD + CB])
        total = sb("total", [P, 4, 2])
        neg_mean = sb("neg_mean", [P, 4, 2])
        squares = sb("squares", [P, 4, 2])
        spent = sb("spent", [P, 2, DD])
        var = sb("var", [P, 4, 2])
        var_eps = sb("var_eps", [P, 4, 2])
        rstd = sb("rstd", [P, 4, 2])
        g = sb("g", [P, 4, 2, DD])
        rf = sb("rf", [2 * NB, T, DD])
        rb2 = sb("rb2", [2 * NB, T, DD])
        ra0, rb0 = xT[0:2 * NB, :, :], xbT[0:2 * NB, :, :]
        w_grad, w_grad2, w_z = (sb(n, [2 * NB, 4]) for n in ("w_grad", "w_grad2", "w_z"))
        dt2 = sb("dt2", [2 * NB, 1])
        halfX, halfY = g[:, 0:2, :, :], g[:, 2:4, :, :]
        flat = lambda v: v.rearrange("p a b d -> p (a b d)")
        downN = U[:, 0, :, :].rearrange("p t h -> p (t h)")[:, 0:DD]
        upN = U[:, 1, :, :].rearrange("p t h -> p (t h)")[:, 0:DD]
        vec_a = V[:, 0, 0, 0:P]
        vec_b = V[:, 1, 0, 0:P]
        expert = sb("expert", [A, 2, A])
        idx_i = sb("idx_i", [1, NB], i32)
        idx_w = sb("idx_w", [1, 4, NB])

        x_ps = [pb(f"x_ps{n}", [P, S]) for n in range(2)]
        h_ps = pb("h_ps", [A, S])
        y_ps = [pb(f"y_ps{n}", [P, DD]) for n in range(T)]

        names = ("grid_in small_in border_in vecs_in zeroed seeded wide_ready down_in up_in "
                 "half_ready coef_ready edge_ready weights_t weights_ready vec_sum vec_t vec_ready bias_ps bias_ready "
                 "comb_ps_ready comb_sb_ready border_step ghosts_ready idx_step rows_ready "
                 "u_ready z_done d_done xp_done edge_parts edges_done xm_done uv_done y_done "
                 "x_ready x_taken xb_ready h_ready hid_ready y_ready total_done mean_done squares_done g_done var_done ve_done rstd_ready out_ready")
        s = {n: sem(n) for n in names.split()}
        f_in = [sem(f"f_in{k}") for k in range(2)]
        comb_in = [sem(f"comb_in{k}") for k in range(2)]
        expert_in = [sem(f"expert_in{k}") for k in range(2)]
        comb_stored = [sem(f"comb_stored{k}") for k in range(2)]
        stored = [sem(f"stored{n}") for n in range(4)]

        def known(n, least=1):
            return not isinstance(n, int) or n >= least

        def batch_loads(b, k):
            return (b - k) * 8 + 16

        batch_combs = batch_loads

        def all_batches(eng, body):
            body(0, 0), body(1, 1)
            with eng.Fori(1, NB // 2 - 1) as i:
                body(i * 2, 0)
                body(i * 2 + 1, 1)
            body(NB - 2, 0), body(NB - 1, 1)

        def pair_of(b, k, h, back):
            q = b * 2 + (h - back)
            return (q, (2 * k + h - back) % 4) if known(q, 0) else None

        block = ctx.enter_context(nc.Block())

        @block.sync
        def _(sp):
            sp.dma_start(c_ym[:, :, :], grid_v[0][1]).then_inc(s["grid_in"], 16)
            sp.dma_start(c_yp[:, :, :], grid_v[1][1]).then_inc(s["grid_in"], 16)
            sp.dma_start(c_xp[:, :, :], grid_v[1][0]).then_inc(s["grid_in"], 16)
            sp.dma_start(c_xm[:, :, :], grid_v[0][0]).then_inc(s["grid_in"], 16)
            sp.dma_start(c_z[:, :, :], grid_v[1][2]).then_inc(s["grid_in"], 16)
            sp.dma_start(f[:, 0, :, :], x_v[0]).then_inc(f_in[0], 16)
            sp.dma_start(f[:, 1, :, :], x_v[1]).then_inc(f_in[1], 16)
            for side, r0 in ((0, 0), (1, S - 4)):
                p0, p1 = side * NB, (side + 1) * NB
                sp.dma_start(rf[p0:p1, :, :], x[:, r0:r0 + 4, :]).then_inc(s["border_in"], 16)
                sp.dma_start(dt2[p0:p1, :], dt_b.rearrange("(b a) -> b a", a=1)).then_inc(s["border_in"], 16)
                for dst, src in ((ra0[p0:p1], A_grid[0]), (rb0[p0:p1], B_grid[0]), (rb2[p0:p1, :, :], B_grid[2])):
                    sp.dma_start(dst, src[r0:r0 + 4, :].partition_broadcast(NB)).then_inc(s["border_in"], 16)

            def expert_loads(i, k):
                if known(i):
                    sp.wait_ge(s["comb_ps_ready"], i * 2 + (k - 1))
                sp.dma_start(expert[:, k, :], expert_W[i * 2 + k]).then_inc(expert_in[k], 16)

            def comb_stores(i, k):
                sp.wait_ge(s["comb_sb_ready"], i * 2 + (k + 1))
                sp.dma_start(comb_dram[i * 2 + k], comb[:, k, :]).then_inc(comb_stored[k], 16)

            for k in range(2):
                expert_loads(0, k)
            with sp.Fori(1, E // 2) as i:
                for k in range(2):
                    expert_loads(i, k)
                    comb_stores(i - 1, k)
            for k in range(2):
                comb_stores(E // 2 - 1, k)
            for k in range(2):
                comb_stores(E // 2, k)
            for k in range(2):
                sp.wait_ge(comb_stored[k], 16 * (E // 2 + 1))
            sp.wait_ge(s["rows_ready"], 1)

            def load_comb(b, k):
                e = sp.value_load(rows[0:1, bass.ds(b, 1)], min_val=0, max_val=ROWS - 1)
                sp.dma_start(comb[:, k, :], comb_dram[bass.ds(e, 1), :, :].rearrange("a p d -> p (a d)")).then_inc(comb_in[k], 16)

            load_comb(0, 0)

            def store_pair(q, slot):
                b2, th = q
                n = slot
                src = g[:, n, :, :].rearrange("p a d -> p (a d)")
                sp.dma_start(out_v[bass.ds(b2, 1), :, th * 2 * DD:(th + 1) * 2 * DD].rearrange("a p d -> p (a d)"),
                             src).then_inc(stored[n], 16)

            def body(b, k):
                last = isinstance(b, int) and b == NB - 1
                if not last:
                    if known(b):
                        sp.wait_ge(s["x_ready"], b * CB)
                        sp.dma_start(f[:, 1 - k, :, :], x_v[bass.ds(b + 1, 1), :, :].rearrange("a p d -> p (a d)")
                                     ).then_inc(f_in[1 - k], 16)
                        sp.wait_ge(s["y_ready"], b * T)
                    load_comb(b + 1, 1 - k)
                if known(b, 2):
                    for th in range(2):
                        sp.wait_ge(s["out_ready"], (b - 2) * 2 + (th + 1))
                        store_pair((b - 2, th), (2 * k + th) % 4)

            all_batches(sp, body)
            for b in (NB - 2, NB - 1):
                for th in range(2):
                    sp.wait_ge(s["out_ready"], 2 * b + th + 1)
                    store_pair((b, th), (2 * b + th) % 4)
            for n in range(4):
                sp.wait_ge(stored[n], 16 * (NB // 2))

        @block.gpsimd
        def _(pool):
            pool.memset(wide[:, :], 0.0).then_inc(s["seeded"], 1)
            for tile, value in ((minus_half, -0.5), (one_over_d, 1.0 / DD), (eps, EPS)):
                pool.memset(tile[:, :], value).then_inc(s["seeded"], 1)
            pool.wait_ge(s["seeded"], 1)
            pool.affine_select(out=wide[:, :], in_=wide[:, :], compare_op=ALU.not_equal, fill=1.0,
                               base=2, pattern=[[-1, P + 4]], channel_multiplier=1).then_inc(s["wide_ready"], 1)
            pool.wait_ge(s["coef_ready"], 6)
            pool.wait_ge(s["vec_t"], 1)

            def products(b, k, h):
                J = slice(H * h, H * h + H)
                pool.wait_ge(s["u_ready"], b + 1)
                if known(b):
                    pool.wait_ge(s["x_ready"], (b - 1) * CB + (2 * h + 2))
                pool.tensor_tensor(out=V[:, h, :, :], in0=u[:, k, :, J], in1=c_xm[:, :, J], op=ALU.mult).then_inc(s["xm_done"], 1)
                q = pair_of(b, k, h, 4)
                if q:
                    inverse_deviation(*q)
                a, lo, n = (1, 0, H - 1) if h == 0 else (0, H - 1, H)
                pool.tensor_tensor(out=Ym[:, h, :, a:a + n], in0=u[:, k, :, lo:lo + n], in1=c_ym[:, :, lo:lo + n], op=ALU.mult)
                lo, n = (1, H) if h == 0 else (H + 1, H - 1)
                pool.tensor_tensor(out=Yp[:, h, :, 0:n], in0=u[:, k, :, lo:lo + n], in1=c_yp[:, :, lo:lo + n], op=ALU.mult)
                pool.tensor_tensor(out=C[:, h, :, :], in0=u[:, k, :, J], in1=c_c[:, :, J], op=ALU.mult).then_inc(s["y_done"], 1)

            def inverse_deviation(q, n):
                pool.wait_ge(s["squares_done"], q * 2 + 2)
                pool.tensor_tensor(out=var[:, n, :], in0=squares[:, n, :], in1=one_over_d[:, :], op=ALU.mult).then_inc(s["var_done"], 1)
                pool.wait_ge(s["var_done"], q + 1)
                pool.tensor_tensor(out=var_eps[:, n, :], in0=var[:, n, :], in1=eps[:, :], op=ALU.add).then_inc(s["ve_done"], 1)
                pool.wait_ge(s["ve_done"], q + 1)
                pool.tensor_tensor(out=rstd[:, n, :], in0=var_eps[:, n, :], in1=minus_half[:, :], op=ALU.pow).then_inc(s["rstd_ready"], 1)

            def body(b, k):
                for h in range(2):
                    products(b, k, h)

            all_batches(pool, body)
            for q in range(2 * NB - 4, 2 * NB):
                inverse_deviation(q, q % 4)

        @block.scalar
        def _(act):
            act.dma_start(downN, down_W).then_inc(s["down_in"], 16)
            act.dma_start(upN.rearrange("p (c a) -> p c a", c=CB), up_W.rearrange("(c p) a -> p c a", p=P)).then_inc(s["up_in"], 16)
            act.dma_start(dts[:, :], dt_b.partition_broadcast(P)).then_inc(s["small_in"], 16)
            act.dma_start(idx_i[:, :], expert_id.rearrange("(a b) -> a b", a=1)).then_inc(s["small_in"], 16)
            act.dma_start(gamma[:, :], ln_gamma.partition_broadcast(P)).then_inc(s["small_in"], 16)
            act.dma_start(beta[:, :], ln_beta.partition_broadcast(P)).then_inc(s["small_in"], 16)
            act.wait_ge(s["zeroed"], 3)
            act.dma_start(vec_a[0:E, :], expert_b).then_inc(s["vecs_in"], 16)
            act.dma_start(vec_b[0:E, :], domain_emb).then_inc(s["vecs_in"], 16)
            act.dma_start(vec_b[KEEP0:KEEP0 + 1, :], domain_emb[0:1, :]).then_inc(s["vecs_in"], 16)
            act.dma_start(vec_b[KEEPN:KEEPN + 1, :], domain_emb[E - 1:E, :]).then_inc(s["vecs_in"], 16)
            act.dma_start(vec_b[V_UPB:V_UPB + CB, :], up_b.rearrange("(c p) -> c p", p=P)).then_inc(s["vecs_in"], 16)
            act.dma_start(vec_b[V_DOWNB:V_DOWNB + 1, :], down_b.rearrange("(a p) -> a p", a=1)).then_inc(s["vecs_in"], 16)

            act.wait_ge(s["grid_in"], 80)
            act.activation(flat(halfY), c_yp[:, :, :].rearrange("p t d -> p (t d)"), ACT.Copy, scale=0.5).then_inc(s["half_ready"], 1)
            act.activation(flat(halfX), c_xp[:, :, :].rearrange("p t d -> p (t d)"), ACT.Copy, scale=0.5).then_inc(s["half_ready"], 1)

            def scale_by_dt(b, k):
                act.wait_ge(f_in[k], batch_loads(b, k))
                if known(b, 2):
                    act.wait_ge(s["uv_done"], (b - 1) * 2)
                    act.wait_ge(s["y_done"], (b - 1) * 2)
                act.activation(u[:, k, :, :].rearrange("p t d -> p (t d)"), f[:, k, :, :].rearrange("p t d -> p (t d)"),
                               ACT.Copy, scale=dts[:, bass.ds(b, 1)]).then_inc(s["u_ready"], 1)

            act.wait_ge(s["weights_t"], 1)
            act.activation(downT[:, :, :].rearrange("p c a -> p (c a)"), x_ps[0][:, :], ACT.Copy).then_inc(s["weights_ready"], 1)
            act.wait_ge(s["weights_t"], 2)
            act.activation(upT[:, :], x_ps[1][:, :], ACT.Copy).then_inc(s["weights_ready"], 1)
            act.wait_ge(s["vec_t"], 1)
            act.activation(vecT[:, :], h_ps[:, 0:P], ACT.Copy).then_inc(s["vec_ready"], 1)
            act.wait_ge(s["vec_ready"], 1)
            act.wait_ge(s["bias_ps"], 1)
            for c in range(CB):
                act.activation(biasT[:, c, :], y_ps[0][:, c * P:c * P + ROWS], ACT.Identity,
                               bias=vecT[:, V_UPB + c:V_UPB + c + 1]).then_inc(s["bias_ready"], 1)
            act.wait_ge(s["bias_ready"], CB)
            act.wait_ge(s["small_in"], 64)
            scale_by_dt(0, 0)

            def comb_out(i, k, src):
                if known(i):
                    act.wait_ge(comb_stored[k], i * 16)
                act.activation(comb[:, k, DD:DD + CB], biasT[:, :, bass.ds(i * 2 + k, 1)].rearrange("p c a -> p (c a)"), ACT.Copy)
                act.activation(comb[:, k, 0:DD], src, ACT.Copy).then_inc(s["comb_sb_ready"], 1)

            def comb_row(i, k):
                act.wait_ge(s["comb_ps_ready"], i * 2 + (k + 1))
                comb_out(i, k, y_ps[2 + k][:, :])

            for k in range(2):
                comb_row(0, k)
            with act.Fori(1, E // 2) as i:
                for k in range(2):
                    comb_row(i, k)
            for k in range(2):
                comb_out(E // 2, k, upT[:, :])

            def statistics(q, n):
                if known(q):
                    act.wait_ge(s["squares_done"], q * 2)
                for j in range(2):
                    act.wait_ge(s["y_ready"], q * 2 + (j + 1))
                    act.activation(spent[:, j, :], y_ps[2 * (n % 2) + j][:, :], ACT.Identity,
                                   accum_out=total[:, n, j:j + 1]).then_inc(s["total_done"], 1)
                act.wait_ge(s["total_done"], q * 2 + 2)
                act.activation(neg_mean[:, n, :], total[:, n, :], ACT.Copy, scale=-1.0 / DD).then_inc(s["mean_done"], 1)
                act.wait_ge(s["mean_done"], q + 1)
                for j in range(2):
                    act.activation(spent[:, j, :], y_ps[2 * (n % 2) + j][:, :], ACT.Square, bias=neg_mean[:, n, j:j + 1],
                                   accum_out=squares[:, n, j:j + 1]).then_inc(s["squares_done"], 1)

            def body(b, k):
                last = isinstance(b, int) and b == NB - 1
                if not last:
                    scale_by_dt(b + 1, 1 - k)
                if known(b):
                    act.wait_ge(s["h_ready"], b + 0)
                    act.wait_ge(s["xb_ready"], b * CB)
                for c in range(CB):
                    act.wait_ge(s["x_ready"], b * CB + (c + 1))
                    if isinstance(b, int) and b == 0 and c == 0:
                        act.wait_ge(s["ghosts_ready"], 1)
                    act.activation(xT[:, c, :], x_ps[c % 2][:, :], ACT.Relu).then_inc(s["x_taken"], 1)
                    if c % 2:
                        q = pair_of(b, k, c // 2, 3)
                        if q:
                            statistics(*q)
                act.wait_ge(comb_in[k], batch_combs(b, k))
                if known(b):
                    act.wait_ge(s["y_ready"], b * T)
                act.wait_ge(s["x_taken"], b * CB + CB)
                for c in range(CB):
                    act.activation(xbT[:, c, :], xT[:, c, :], ACT.Identity,
                                   bias=comb[:, k, DD + c:DD + c + 1]).then_inc(s["xb_ready"], 1)
                act.wait_ge(s["h_ready"], b + 1)
                act.activation(hT[:, :], h_ps[:, :], ACT.Gelu, bias=vecT[:, V_DOWNB:V_DOWNB + 1]).then_inc(s["hid_ready"], 1)

            all_batches(act, body)
            for q in range(2 * NB - 3, 2 * NB):
                statistics(q, q % 4)

        @block.tensor
        def _(pe):
            pe.wait_ge(s["wide_ready"], 1)
            pe.wait_ge(s["down_in"], 16)
            for c in range(CB):
                last = pe.transpose(x_ps[0][:, c * P:c * P + P], downN[:, c * P:c * P + P], ident)
            last.then_inc(s["weights_t"], 1)
            pe.wait_ge(s["up_in"], 16)
            for c in range(CB):
                last = pe.transpose(x_ps[1][:, c * P:c * P + P], upN[:, c * P:c * P + P], ident)
            last.then_inc(s["weights_t"], 1)
            pe.wait_ge(s["vec_sum"], 1)
            pe.transpose(h_ps[:, 0:P], vec_a, ident).then_inc(s["vec_t"], 1)
            pe.wait_ge(s["weights_ready"], 2)
            pe.wait_ge(s["vec_ready"], 1)
            for c in range(CB):
                last = pe.matmul(y_ps[0][:, c * P:c * P + ROWS], upT[:, c * P:c * P + P], vecT[:, 0:ROWS], start=True, stop=True)
            last.then_inc(s["bias_ps"], 1)

            def comb_row(i, k):
                pe.wait_ge(expert_in[k], i * 16 + 16)
                if known(i):
                    pe.wait_ge(s["comb_sb_ready"], i * 2 + (k - 1))
                pe.matmul(y_ps[2 + k][:, :], expert[:, k, :], upT[:, :], start=True, stop=True).then_inc(s["comb_ps_ready"], 1)

            for k in range(2):
                comb_row(0, k)
            with pe.Fori(1, E // 2) as i:
                for k in range(2):
                    comb_row(i, k)

            def stencil(b, k, h):
                if h == 0:
                    pe.wait_ge(f_in[k], batch_loads(b, k))
                pe.wait_ge(s["y_done"], b * 2 + (h + 1))
                pe.wait_ge(s["uv_done"], b * 2 + (h + 1))
                for c in (2 * h, 2 * h + 1):
                    if known(b) or c >= 2:
                        pe.wait_ge(s["x_taken"], b * CB + (c - 1))
                    bank, cols, loc = x_ps[c % 2], slice(c * P, c * P + P), slice((c % 2) * P, (c % 2) * P + P)

                    def add(term, t_out, shift=None, start=False):
                        pe.matmul(bank[:, t_out * P:t_out * P + P], term, ident if shift is None else shift, start=start, stop=False,
                                  is_transpose=(shift is None), skip_group_check=True)

                    for t in range(T):
                        add(f[:, k, t, cols], t, start=(t == 0))
                    for t in range(T):
                        add(C[:, h, t, loc], t)
                    for t in range(T):
                        add(Yp[:, h, t, loc], t)
                    for t in range(T):
                        add(Ym[:, h, t, loc], t)
                    for t in range(T):
                        add(U[:, h, t, loc], (t - 1) % T, shift_up if t == 0 else None)
                    for t in range(T):
                        add(V[:, h, t, loc], (t + 1) % T, shift_down if t == T - 1 else None)
                    if isinstance(b, int) and b == 0 and c == 0:
                        pe.wait_ge(s["ghosts_ready"], 1)
                    pick = wide[:, 2:P + 2].rearrange("p (s b) -> p b s", b=NB)[:, bass.ds(b, 1), 0:2].rearrange("p a s -> p (a s)")
                    pe.matmul(bank[:, 0:S:S - 1], ghosts[:, cols], pick, start=False, stop=True,
                              skip_group_check=True).then_inc(s["x_ready"], 1)

            def up(b, k, th):
                for t in (2 * th, 2 * th + 1):
                    if t == 0:
                        pe.wait_ge(s["hid_ready"], b + 1)
                        pe.wait_ge(comb_in[k], batch_combs(b, k))
                        pe.wait_ge(s["xb_ready"], b * CB + CB)
                    if known(b):
                        pe.wait_ge(s["g_done"], (b - 1) * T + (t + 1))
                    pe.matmul(y_ps[t][:, :], hT[:, t * P:t * P + P], comb[:, k, 0:DD], start=True, stop=False, skip_group_check=True)
                    for c in range(CB):
                        last = pe.matmul(y_ps[t][:, c * P:c * P + P], xbT[:, c, t * P:t * P + P], ident, start=False,
                                         stop=(c == CB - 1), is_transpose=True, skip_group_check=True)
                    last.then_inc(s["y_ready"], 1)

            def down(b):
                pe.wait_ge(s["x_taken"], b * CB + CB)
                if known(b):
                    pe.wait_ge(s["hid_ready"], b + 0)
                for c in range(CB):
                    last = pe.matmul(h_ps[:, :], downT[:, c, :], xT[:, c, :], start=(c == 0), stop=(c == CB - 1))
                last.then_inc(s["h_ready"], 1)

            def body(b, k):
                for h in range(2):
                    stencil(b, k, h)
                    if known(b):
                        up(b - 1, 1 - k, h)
                down(b)

            all_batches(pe, body)
            for th in range(2):
                up(NB - 1, 1, th)

        @block.vector
        def _(dve):
            dve.memset(vec_a, 0.0).then_inc(s["zeroed"], 1)
            dve.memset(vec_b, 0.0).then_inc(s["zeroed"], 1)
            dve.memset(ghosts[:, :], 0.0).then_inc(s["zeroed"], 1)
            for r in range(4):
                for w, first, last, scale in ((w_grad, GRAD[r], -GRAD[3 - r], 0.5), (w_grad2, GRAD2[r], GRAD2[3 - r], 0.5),
                                              (w_z, GRAD[r], -GRAD[3 - r], 0.25)):
                    dve.memset(w[0:NB, r:r + 1], first * scale)
                    dve.memset(w[NB:2 * NB, r:r + 1], last * scale).then_inc(s["border_step"], 1)
            n_border = [12]

            dve.wait_ge(s["small_in"], 64)
            dve.tensor_scalar(idx_w[:, 0, :], idx_i[:, :], 0.0, float(E - 1), ALU.max, ALU.min).then_inc(s["idx_step"], 1)
            dve.tensor_scalar(idx_w[:, 1, :], idx_i[:, :], 0.0, float(KEEP0), ALU.is_lt, ALU.mult).then_inc(s["idx_step"], 1)
            dve.tensor_scalar(idx_w[:, 2, :], idx_i[:, :], float(E - 1), float(KEEPN - (E - 1)), ALU.is_gt, ALU.mult).then_inc(s["idx_step"], 1)
            dve.wait_ge(s["idx_step"], 3)
            dve.tensor_tensor(out=idx_w[:, 3, :], in0=idx_w[:, 0, :], in1=idx_w[:, 1, :], op=ALU.add).then_inc(s["idx_step"], 1)
            dve.wait_ge(s["idx_step"], 4)
            dve.tensor_tensor(out=rows[:, :], in0=idx_w[:, 3, :], in1=idx_w[:, 2, :], op=ALU.add).then_inc(s["rows_ready"], 1)

            dve.wait_ge(s["vecs_in"], 96)
            dve.tensor_tensor(out=vec_a, in0=vec_a, in1=vec_b, op=ALU.add).then_inc(s["vec_sum"], 1)

            dve.wait_ge(s["grid_in"], 80)
            n_edge = 0
            for side in range(2):
                for j in range(4):
                    r = j if side == 0 else 3 - j
                    col = j if side == 0 else DD - 4 + j
                    sign = 1.0 if side == 0 else -1.0
                    w = c_yghost[:, side, :, j]
                    dve.tensor_scalar(w, c_yp[:, :, col], 0.5 * GRAD2[r], None, ALU.mult).then_inc(s["edge_ready"], 1)
                    n_edge += 1
                    if GRAD[r]:
                        dve.wait_ge(s["edge_ready"], n_edge)
                        dve.scalar_tensor_tensor(out=w, in0=c_ym[:, :, col], scalar=0.5 * sign * GRAD[r], in1=w,
                                                 op0=ALU.mult, op1=ALU.add).then_inc(s["edge_ready"], 1)
                        n_edge += 1
                for j in range(3):
                    r = j if side == 0 else 2 - j
                    col = j if side == 0 else DD - 3 + j
                    sign = 1.0 if side == 0 else -1.0
                    dve.tensor_scalar(c_dedge[:, side, :, j], c_z[:, :, col], 0.25 * sign * EDGE[r], None, ALU.mult).then_inc(s["edge_ready"], 1)
                    n_edge += 1
            dve.wait_ge(s["edge_ready"], n_edge)

            dve.scalar_tensor_tensor(out=c_c[:, :, :], in0=c_xp[:, :, :], scalar=-1.0, in1=c_yp[:, :, :],
                                     op0=ALU.mult, op1=ALU.subtract).then_inc(s["coef_ready"], 1)
            dve.tensor_scalar(c_z[:, :, :], c_z[:, :, :], 0.25, None, ALU.mult).then_inc(s["coef_ready"], 1)
            dve.wait_ge(s["coef_ready"], 2)
            for n, (plus, minus, half) in enumerate(((c_yp, c_ym, halfY), (c_xp, c_xm, halfX))):
                dve.wait_ge(s["half_ready"], n + 1)
                hv = half.rearrange("p a b d -> p (a b) d")
                dve.scalar_tensor_tensor(out=plus[:, :, :], in0=minus[:, :, :], scalar=-0.5, in1=hv,
                                         op0=ALU.mult, op1=ALU.add).then_inc(s["coef_ready"], 1)
                dve.wait_ge(s["coef_ready"], 3 + 2 * n)
                dve.scalar_tensor_tensor(out=minus[:, :, :], in0=minus[:, :, :], scalar=0.5, in1=hv,
                                         op0=ALU.mult, op1=ALU.add).then_inc(s["coef_ready"], 1)
            dve.wait_ge(s["coef_ready"], 6)

            def row_ghosts():
                R = 2 * NB

                def step(ins):
                    ins.then_inc(s["border_step"], 1)
                    n_border[0] += 1

                def settle():
                    dve.wait_ge(s["border_step"], n_border[0])

                dve.wait_ge(s["border_in"], 160)
                settle()
                step(dve.tensor_scalar(rf[:, :, :], rf[:, :, :], dt2[:, :], None, ALU.mult))
                settle()
                for r in range(4):
                    step(dve.scalar_tensor_tensor(out=rb2[:, r, :], in0=rb2[:, r, :], scalar=w_z[:, r:r + 1], in1=rf[:, r, :],
                                                  op0=ALU.mult, op1=ALU.mult))
                    step(dve.scalar_tensor_tensor(out=ra0[:, r, :], in0=ra0[:, r, :], scalar=w_grad[:, r:r + 1], in1=rf[:, r, :],
                                                  op0=ALU.mult, op1=ALU.mult))
                    step(dve.scalar_tensor_tensor(out=rb0[:, r, :], in0=rb0[:, r, :], scalar=w_grad2[:, r:r + 1], in1=rf[:, r, :],
                                                  op0=ALU.mult, op1=ALU.mult))
                settle()
                step(dve.tensor_tensor(out=ra0[:, :, :], in0=ra0[:, :, :], in1=rb0[:, :, :], op=ALU.add))
                step(dve.tensor_tensor(out=rb2[:, 0:2, :], in0=rb2[:, 0:2, :], in1=rb2[:, 2:4, :], op=ALU.add))
                settle()
                step(dve.tensor_tensor(out=ra0[:, 0:2, :], in0=ra0[:, 0:2, :], in1=ra0[:, 2:4, :], op=ALU.add))
                step(dve.tensor_tensor(out=rb2[:, 0, :], in0=rb2[:, 0, :], in1=rb2[:, 1, :], op=ALU.add))
                settle()
                step(dve.tensor_tensor(out=ra0[:, 0, :], in0=ra0[:, 0, :], in1=ra0[:, 1, :], op=ALU.add))
                z, d = rb2[:, 0, :], rb2[:, 2, :]
                step(dve.tensor_tensor(out=d[:, 1:DD - 1], in0=z[:, 0:DD - 2], in1=z[:, 2:DD], op=ALU.subtract))
                for col, j1, j2, sign in ((0, 1, 2, 1.0), (DD - 1, DD - 2, DD - 3, -1.0)):
                    e = d[:, col:col + 1]
                    step(dve.tensor_scalar(e, z[:, col:col + 1], -sign * EDGE[0], None, ALU.mult))
                    settle()
                    for jj, wgt in ((j1, EDGE[1]), (j2, EDGE[2])):
                        step(dve.scalar_tensor_tensor(out=e, in0=z[:, jj:jj + 1], scalar=-sign * wgt, in1=e, op0=ALU.mult, op1=ALU.add))
                        settle()
                dve.wait_ge(s["zeroed"], 3)
                dve.tensor_tensor(out=ghosts[0:R, :], in0=ra0[:, 0, :], in1=d, op=ALU.add).then_inc(s["ghosts_ready"], 1)

            def row_terms(b, k, h):
                n = b * 2 + h
                J = slice(H * h, H * h + H)
                dve.wait_ge(s["u_ready"], b + 1)
                if known(b):
                    dve.wait_ge(s["x_ready"], (b - 1) * CB + (2 * h + 2))
                z0, z1 = (0, H + 1) if h == 0 else (H + 1, DD)
                dve.tensor_tensor(out=Z[:, :, z0:z1], in0=u[:, k, :, z0:z1], in1=c_z[:, :, z0:z1], op=ALU.mult).then_inc(s["z_done"], 1)
                e4, e3 = ((0, 4), (0, 3)) if h == 0 else ((DD - 4, DD), (DD - 3, DD))
                dve.tensor_tensor(out=yg_part[:, h, :, :], in0=u[:, k, :, e4[0]:e4[1]], in1=c_yghost[:, h, :, :], op=ALU.mult)
                dve.tensor_tensor(out=de_part[:, h, :, :], in0=u[:, k, :, e3[0]:e3[1]], in1=c_dedge[:, h, :, :], op=ALU.mult).then_inc(s["edge_parts"], 1)
                dve.tensor_tensor(out=U[:, h, :, :], in0=u[:, k, :, J], in1=c_xp[:, :, J], op=ALU.mult).then_inc(s["xp_done"], 1)
                dve.wait_ge(s["z_done"], n + 1)
                if h == 0:
                    dve.tensor_tensor(out=D[:, :, 1:H], in0=Z[:, :, 2:H + 1], in1=Z[:, :, 0:H - 1], op=ALU.subtract).then_inc(s["d_done"], 1)
                else:
                    dve.tensor_tensor(out=D[:, :, 0:H - 1], in0=Z[:, :, H + 1:DD], in1=Z[:, :, H - 1:DD - 2], op=ALU.subtract).then_inc(s["d_done"], 1)
                dve.wait_ge(s["edge_parts"], n + 1)
                ghost, edge = (Ym[:, h, :, 0:1], D[:, :, 0:1]) if h == 0 else (Yp[:, h, :, H - 1:H], D[:, :, H - 1:H])
                dve.tensor_reduce(ghost, yg_part[:, h, :, :], AX.X, ALU.add)
                dve.tensor_reduce(edge, de_part[:, h, :, :], AX.X, ALU.add).then_inc(s["edges_done"], 1)
                dve.wait_ge(s["d_done"], n + 1)
                dve.wait_ge(s["xp_done"], n + 1)
                dve.wait_ge(s["edges_done"], n + 1)
                dve.tensor_tensor(out=U[:, h, :, :], in0=U[:, h, :, :], in1=D[:, :, :], op=ALU.add)
                dve.wait_ge(s["xm_done"], n + 1)
                dve.tensor_tensor(out=V[:, h, :, :], in0=V[:, h, :, :], in1=D[:, :, :], op=ALU.subtract).then_inc(s["uv_done"], 1)

            def centre(q, n):
                if known(q, 4):
                    dve.wait_ge(stored[n], (q - n) * 4)
                for j in range(2):
                    dve.wait_ge(s["squares_done"], q * 2 + (j + 1))
                    dve.scalar_tensor_tensor(out=g[:, n, j, :], in0=y_ps[2 * (n % 2) + j][:, :], scalar=neg_mean[:, n, j:j + 1],
                                             in1=gamma[:, :], op0=ALU.add, op1=ALU.mult).then_inc(s["g_done"], 1)

            def finish(q, n):
                dve.wait_ge(s["rstd_ready"], q + 1)
                dve.wait_ge(s["g_done"], q * 2 + 2)
                for j in range(2):
                    last = dve.scalar_tensor_tensor(out=g[:, n, j, :], in0=g[:, n, j, :], scalar=rstd[:, n, j:j + 1], in1=beta[:, :],
                                                    op0=ALU.mult, op1=ALU.add)
                last.then_inc(s["out_ready"], 1)

            def norm_slot(b, k, h):
                for back, what in ((3, centre), (4, finish)):
                    q = pair_of(b, k, h, back)
                    if q:
                        what(*q)

            def body(b, k):
                for h in range(2):
                    row_terms(b, k, h)
                    if isinstance(b, int) and (b, h) == (0, 0):
                        row_ghosts()
                    norm_slot(b, k, h)

            dve.wait_ge(s["weights_t"], 2)
            all_batches(dve, body)
            for m in range(4):
                q = 2 * NB - 3 + m
                if q < 2 * NB:
                    centre(q, q % 4)
                finish(q - 1, (q - 1) % 4)


_INS = ['x', 'condB_dt', 'itok_B_0_15', 'L0_cond_A_grid', 'L0_cond_B_grid', 'L1_cond_down_W', 'L1_cond_down_b',
        'L1_cond_up_W', 'L1_cond_up_b', 'L1_cond_expert_W', 'L1_cond_expert_b', 'L1_cond_domain_emb',
        'L1_cond_ln_gamma', 'L1_cond_ln_beta']


def kernel(**inputs):
    import numpy as _np
    import concourse.bacc as _bacc
    from concourse import mybir as _mybir
    from concourse.bass_utils import run_bass_kernel_spmd as _run

    nc = _bacc.Bacc("TRN2", target_bir_lowering=False, num_devices=1)
    arrays, args = {}, []
    for name in _INS:
        a = _np.ascontiguousarray(inputs[name])
        arrays[f"in_{name}_dram"] = a
        args.append(nc.dram_tensor(f"in_{name}_dram", a.shape, _mybir.dt.from_np(a.dtype), kind="ExternalInput").ap())
    args.append(nc.dram_tensor("out_0_dram", inputs["x"].shape, _mybir.dt.float32, kind="ExternalOutput").ap())
    stencil_adapter_kernel(nc, *args)
    r = _run(nc, [arrays], core_ids=[0])
    return r.results[0]["out_0_dram"]
```

```python
import concourse.bass as bass
from concourse import mybir
from contextlib import ExitStack


def stencil_adapter_kernel(nc, x, dt_b, expert_id, A_grid, B_grid, down_W, down_b, up_W, up_b,
                           expert_W, expert_b, domain_emb, ln_gamma, ln_beta, out):
    fp32, i32 = mybir.dt.float32, mybir.dt.int32
    ALU, ACT, AX = mybir.AluOpType, mybir.ActivationFunctionType, mybir.AxisListType

    NB, S, DD = x.shape
    A, E = down_b.shape[0], expert_b.shape[0]
    P = 128
    T = S // P
    CB = DD // P
    H = DD // 2
    R = 4
    EDGE_OPS = 20
    LEAD = 4
    EPS = 1e-5
    KEEP0, KEEPN, ROWS = E, E + 1, E + 2
    V_UPB, V_DOWNB = ROWS, ROWS + CB
    GRAD = (3.0, -3.0, 1.0, 0.0)
    GRAD2 = (4.0, -6.0, 4.0, -1.0)
    EDGE = (-3.0, 4.0, -1.0)

    x_v = x.rearrange("b (p t) d -> b p (t d)", t=T)
    out_v = out.rearrange("b (p t) d -> b p (t d)", t=T)
    grid_v = [g.rearrange("c (p t) d -> c p t d", t=T) for g in (A_grid, B_grid)]
    comb_dram = nc.dram_tensor("comb_dram", [ROWS, P, DD + CB], fp32, kind="Internal").ap()

    ctx = ExitStack()
    with ctx:
        def sb(name, shape, dt=fp32):
            return ctx.enter_context(nc.sbuf_tensor(name, shape, dt))

        def pb(name, shape):
            return ctx.enter_context(nc.psum_tensor(name, shape, fp32))

        def sem(name):
            return ctx.enter_context(nc.semaphore(name))

        c_xp, c_xm, c_yp, c_ym, c_c, c_z = (sb(n, [P, T, DD]) for n in ("c_xp", "c_xm", "c_yp", "c_ym", "c_c", "c_z"))
        c_yghost = sb("c_yghost", [P, 2, T, 4])
        c_dedge = sb("c_dedge", [P, 2, T, 3])
        wide = sb("wide", [P, P + 4])
        ident, shift_up, shift_down = wide[:, 2:P + 2], wide[:, 3:P + 3], wide[:, 1:P + 1]
        dts = sb("dts", [P, 2])
        gamma, beta = sb("gamma", [P, DD]), sb("beta", [P, DD])
        downT = sb("downT", [P, CB, A])
        upT = sb("upT", [A, DD])
        vecT = sb("vecT", [P, P])
        biasT = sb("biasT", [P, CB, ROWS])
        rows = sb("rows", [1, NB], i32)
        ghosts = sb("ghosts", [P, DD])
        picks = sb("picks", [P, 2 * NB])
        minus_half, one_over_d, eps = (sb(n, [P, 2]) for n in ("minus_half", "one_over_d", "eps"))
        f = sb("f", [P, 2, T, DD])
        u = sb("u", [P, 2, T, DD])
        U, V, Yp, Ym, C = (sb(n, [P, 2, T, H]) for n in ("U", "V", "Yp", "Ym", "C"))
        Z = sb("Z", [P, T, DD])
        D = sb("D", [P, T, H])
        yg_part = sb("yg_part", [P, 2, T, 4])
        de_part = sb("de_part", [P, 2, T, 3])
        xT = sb("xT", [P, CB, S])
        xbT = sb("xbT", [P, CB, S])
        hT = sb("hT", [A, S])
        comb = sb("comb", [P, 2, DD + CB])
        total = sb("total", [P, 4, 2])
        neg_mean = sb("neg_mean", [P, 4, 2])
        squares = sb("squares", [P, 4, 2])
        spent = sb("spent", [P, 2, DD])
        var = sb("var", [P, 4, 2])
        var_eps = sb("var_eps", [P, 4, 2])
        rstd = sb("rstd", [P, 4, 2])
        g = sb("g", [P, 4, 2, DD])
        rf, rb2 = (sb(n, [P, 2, DD]) for n in ("rf", "rb2"))
        ra0, rb0 = xT[:, 0:2, :], xbT[:, 0:2, :]
        w_grad, w_grad2, w_z = (sb(n, [P, 2]) for n in ("w_grad", "w_grad2", "w_z"))
        dt2 = sb("dt2", [P, 1])
        halfX, halfY = g[:, 0:2, :, :], g[:, 2:4, :, :]
        flat = lambda v: v.rearrange("p a b d -> p (a b d)")
        downN = U[:, 0, :, :].rearrange("p t h -> p (t h)")[:, 0:DD]
        upN = U[:, 1, :, :].rearrange("p t h -> p (t h)")[:, 0:DD]
        vec_a = V[:, 0, 0, 0:P]
        vec_b = V[:, 1, 0, 0:P]
        expert = sb("expert", [A, R, A])
        staged = sb("staged", [P, R, DD + CB])
        idx_i = sb("idx_i", [1, NB], i32)
        idx_w = sb("idx_w", [1, 4, NB])

        x_ps = [pb(f"x_ps{n}", [P, S]) for n in range(2)]
        u_ps = pb("u_ps", [P, T, H])
        y_ps = [pb(f"y_ps{n}", [P, DD]) for n in range(T)]

        names = ("small_in ids_in border_in vecs_in zeroed seeded wide_ready down_in up_in "
                 "half_ready sum_ready c_ready z_ready coef_ready edge_ready weights_t weights_ready vec_sum vec_t vec_ready bias_ps bias_ready "
                 "comb_ps_ready comb_sb_ready border_step ghosts_ready idx_step rows_ready "
                 "picks_ready u_ready u_ps_ready z_done d_done xp_done edge_parts edges_done xm_done uv_done y_done "
                 "x_ready x_taken xb_ready h_ready hid_ready y_ready total_done mean_done squares_done g_done var_done ve_done rstd_ready out_ready")
        s = {n: sem(n) for n in names.split()}
        grid_in = {n: sem(f"grid_in_{n}") for n in ("A0", "B0", "A1", "B1", "B2")}
        f_in = [sem(f"f_in{k}") for k in range(2)]
        comb_in = [sem(f"comb_in{k}") for k in range(2)]
        expert_in = [sem(f"expert_in{k}") for k in range(R)]
        comb_stored = [sem(f"comb_stored{k}") for k in range(R)]
        stored = [sem(f"stored{n}") for n in range(4)]

        def known(n, least=1):
            return not isinstance(n, int) or n >= least

        def batch_loads(b, k):
            return (b - k) * 16 + 32

        def batch_combs(b, k):
            return (b - k) * 8 + 16

        def all_batches(eng, body):
            for b in range(LEAD):
                body(b, b % 2)
            with eng.Fori(LEAD // 2, NB // 2 - 1) as i:
                body(i * 2, 0)
                body(i * 2 + 1, 1)
            body(NB - 2, 0), body(NB - 1, 1)

        def pair_of(b, k, h, back):
            q = b * 2 + (h - back)
            return (q, (2 * k + h - back) % 4) if known(q, 0) else None

        block = ctx.enter_context(nc.Block())

        @block.sync
        def _(sp):
            sp.dma_start(downN, down_W).then_inc(s["down_in"], 16)
            sp.dma_start(upN.rearrange("p (c a) -> p c a", c=CB), up_W.rearrange("(c p) a -> p c a", p=P)).then_inc(s["up_in"], 16)
            sp.wait_ge(s["zeroed"], 2)
            sp.dma_start(vec_a[0:E, :], expert_b).then_inc(s["vecs_in"], 16)
            sp.dma_start(vec_b[0:E, :], domain_emb).then_inc(s["vecs_in"], 16)
            sp.dma_start(vec_b[KEEP0:KEEP0 + 1, :], domain_emb[0:1, :]).then_inc(s["vecs_in"], 16)
            sp.dma_start(vec_b[KEEPN:KEEPN + 1, :], domain_emb[E - 1:E, :]).then_inc(s["vecs_in"], 16)
            sp.dma_start(vec_b[V_UPB:V_UPB + CB, :], up_b.rearrange("(c p) -> c p", p=P)).then_inc(s["vecs_in"], 16)
            sp.dma_start(vec_b[V_DOWNB:V_DOWNB + 1, :], down_b.rearrange("(a p) -> a p", a=1)).then_inc(s["vecs_in"], 16)
            sp.dma_start(idx_i[:, :], expert_id.rearrange("(a b) -> a b", a=1)).then_inc(s["ids_in"], 16)
            for k in range(R):
                sp.dma_start(expert[:, k, :], expert_W[k]).then_inc(expert_in[k], 16)
            sp.dma_start(c_xp[:, :, :], grid_v[1][0]).then_inc(grid_in["B0"], 16)
            sp.dma_start(c_xm[:, :, :], grid_v[0][0]).then_inc(grid_in["A0"], 16)
            sp.dma_start(c_yp[:, :, :], grid_v[1][1]).then_inc(grid_in["B1"], 16)
            sp.dma_start(c_ym[:, :, :], grid_v[0][1]).then_inc(grid_in["A1"], 16)
            sp.dma_start(f[:, 0, :, :], x_v[0]).then_inc(f_in[0], 16)
            sp.dma_start(dts[:, 0:1], dt_b[0:1].partition_broadcast(P)).then_inc(f_in[0], 16)
            sp.dma_start(c_z[:, :, :], grid_v[1][2]).then_inc(grid_in["B2"], 16)
            for m in range(2):
                for side in range(2):
                    r0 = 2 * m + (0, S - 4)[side]
                    p0 = 2 * NB * m + NB * side
                    p1 = p0 + NB
                    sp.dma_start(rf[p0:p1, :, :], x[:, r0:r0 + 2, :]).then_inc(s["border_in"], 16)
                    sp.dma_start(dt2[p0:p1, :], dt_b.rearrange("(b a) -> b a", a=1)).then_inc(s["border_in"], 16)
                    for dst, src in ((ra0[p0:p1], A_grid[0]), (rb0[p0:p1], B_grid[0]), (rb2[p0:p1, :, :], B_grid[2])):
                        sp.dma_start(dst, src[r0:r0 + 2, :].partition_broadcast(NB)).then_inc(s["border_in"], 16)
            sp.dma_start(f[:, 1, :, :], x_v[1]).then_inc(f_in[1], 16)
            sp.dma_start(dts[:, 1:2], dt_b[1:2].partition_broadcast(P)).then_inc(f_in[1], 16)

            def comb_store(i, k):
                sp.wait_ge(s["comb_sb_ready"], i * R + (k + 1))
                sp.dma_start(comb_dram[i * R + k], staged[:, k, :]).then_inc(comb_stored[k], 16)

            with sp.Fori(1, E // R) as i:
                for k in range(R):
                    sp.wait_ge(s["comb_ps_ready"], i * R + (k + 1 - R))
                    sp.dma_start(expert[:, k, :], expert_W[i * R + k]).then_inc(expert_in[k], 16)
                for k in range(R):
                    comb_store(i - 1, k)
            for k in range(R):
                comb_store(E // R - 1, k)
            for k in range(2):
                comb_store(E // R, k)
            for k in range(R):
                sp.wait_ge(comb_stored[k], 16 * (E // R + (k < 2)))
            sp.wait_ge(s["rows_ready"], 1)

            def table_row(b):
                return sp.value_load(rows[0:1, bass.ds(b, 1)], min_val=0, max_val=ROWS - 1)

            def load_comb(e, k):
                sp.dma_start(comb[:, k, :], comb_dram[bass.ds(e, 1), :, :].rearrange("a p d -> p (a d)")).then_inc(comb_in[k], 16)

            load_comb(table_row(0), 0)

            def store_pair(q, slot):
                b2, th = q
                n = slot
                src = g[:, n, :, :].rearrange("p a d -> p (a d)")
                sp.dma_start(out_v[bass.ds(b2, 1), :, th * 2 * DD:(th + 1) * 2 * DD].rearrange("a p d -> p (a d)"),
                             src).then_inc(stored[n], 16)

            def body(b, k):
                last = isinstance(b, int) and b == NB - 1
                if not last:
                    e = table_row(b + 1)
                    if known(b):
                        following = b + 1 if isinstance(b, int) else sp.snap(b + 1)
                        sp.wait_ge(s["x_ready"], b * CB)
                        sp.dma_start(f[:, 1 - k, :, :], x_v[bass.ds(following, 1), :, :].rearrange("a p d -> p (a d)")
                                     ).then_inc(f_in[1 - k], 16)
                        sp.dma_start(dts[:, 1 - k:2 - k], dt_b[bass.ds(following, 1)].partition_broadcast(P)).then_inc(f_in[1 - k], 16)
                        sp.wait_ge(s["y_ready"], b * T)
                    load_comb(e, 1 - k)
                if known(b, 2):
                    for back, th in ((3, 1), (2, 0)):
                        if known(b, back):
                            sp.wait_ge(s["out_ready"], (b - back) * 2 + (th + 1))
                            store_pair((b - back, th), (2 * (k - back) + th) % 4)

            all_batches(sp, body)
            for q in range(2 * NB - 5, 2 * NB):
                sp.wait_ge(s["out_ready"], q + 1)
                store_pair((q // 2, q % 2), q % 4)
            for n in range(4):
                sp.wait_ge(stored[n], 16 * (NB // 2))

        @block.gpsimd
        def _(pool):
            pool.memset(wide[:, :], 0.0).then_inc(s["seeded"], 1)
            for tile, value in ((minus_half, -0.5), (one_over_d, 1.0 / DD), (eps, EPS)):
                pool.memset(tile[:, :], value).then_inc(s["seeded"], 1)
            pool.wait_ge(s["seeded"], 1)
            pool.affine_select(out=wide[:, :], in_=wide[:, :], compare_op=ALU.not_equal, fill=1.0,
                               base=2, pattern=[[-1, P + 4]], channel_multiplier=1).then_inc(s["wide_ready"], 1)
            pool.wait_ge(s["half_ready"], 2)
            pool.tensor_tensor(out=c_c[:, :, :], in0=halfX.rearrange("p a b d -> p (a b) d"), in1=halfY.rearrange("p a b d -> p (a b) d"),
                               op=ALU.add).then_inc(s["sum_ready"], 1)
            pool.wait_ge(s["coef_ready"], 4)


            def products(b, k, h):
                J = slice(H * h, H * h + H)
                pool.wait_ge(s["u_ready"], b + 1)
                if known(b):
                    pool.wait_ge(s["x_ready"], (b - 1) * CB + (2 * h + 2))

                e4, e3 = (slice(0, 4), slice(0, 3)) if h == 0 else (slice(DD - 4, DD), slice(DD - 3, DD))
                if known(b):
                    pool.wait_ge(s["edges_done"], (b - 1) * 2 + (h + 1))
                elif h == 0:
                    pool.wait_ge(s["edge_ready"], EDGE_OPS)
                pool.tensor_tensor(out=yg_part[:, h, :, :], in0=u[:, k, :, e4], in1=c_yghost[:, h, :, :], op=ALU.mult)
                pool.tensor_tensor(out=de_part[:, h, :, :], in0=u[:, k, :, e3], in1=c_dedge[:, h, :, :], op=ALU.mult).then_inc(s["edge_parts"], 1)
                a, lo, n = (1, 0, H - 1) if h == 0 else (0, H - 1, H)
                pool.tensor_tensor(out=Ym[:, h, :, a:a + n], in0=u[:, k, :, lo:lo + n], in1=c_ym[:, :, lo:lo + n], op=ALU.mult)
                q = pair_of(b, k, h, 5)
                if q:
                    inverse_deviation(*q)
                lo, n = (1, H) if h == 0 else (H + 1, H - 1)
                last = pool.tensor_tensor(out=Yp[:, h, :, 0:n], in0=u[:, k, :, lo:lo + n], in1=c_yp[:, :, lo:lo + n], op=ALU.mult)
                if h == 0:
                    if isinstance(b, int) and b == 0:
                        pool.wait_ge(s["c_ready"], 1)
                    last = pool.tensor_tensor(out=C[:, h, :, :], in0=u[:, k, :, J], in1=c_c[:, :, J], op=ALU.mult)
                last.then_inc(s["y_done"], 1)

            def inverse_deviation(q, n):
                pool.wait_ge(s["squares_done"], q * 2 + 2)
                pool.tensor_tensor(out=var[:, n, :], in0=squares[:, n, :], in1=one_over_d[:, :], op=ALU.mult).then_inc(s["var_done"], 1)
                pool.wait_ge(s["var_done"], q + 1)
                pool.tensor_tensor(out=var_eps[:, n, :], in0=var[:, n, :], in1=eps[:, :], op=ALU.add).then_inc(s["ve_done"], 1)
                pool.wait_ge(s["ve_done"], q + 1)
                pool.tensor_tensor(out=rstd[:, n, :], in0=var_eps[:, n, :], in1=minus_half[:, :], op=ALU.pow).then_inc(s["rstd_ready"], 1)

            def body(b, k):
                for h in range(2):
                    products(b, k, h)

            all_batches(pool, body)
            for q in range(2 * NB - 5, 2 * NB):
                inverse_deviation(q, q % 4)

        @block.scalar
        def _(act):



            act.wait_ge(grid_in["B0"], 16)
            act.activation(flat(halfX), c_xp[:, :, :].rearrange("p t d -> p (t d)"), ACT.Copy, scale=0.5).then_inc(s["half_ready"], 1)
            act.wait_ge(grid_in["B1"], 16)
            act.activation(flat(halfY), c_yp[:, :, :].rearrange("p t d -> p (t d)"), ACT.Copy, scale=0.5).then_inc(s["half_ready"], 1)

            def scale_by_dt(b, k):
                act.wait_ge(f_in[k], batch_loads(b, k))
                if known(b, 2):
                    act.wait_ge(s["uv_done"], (b - 1) * 2)
                    act.wait_ge(s["y_done"], (b - 1) * 2)
                act.activation(u[:, k, :, :].rearrange("p t d -> p (t d)"), f[:, k, :, :].rearrange("p t d -> p (t d)"),
                               ACT.Copy, scale=dts[:, k:k + 1]).then_inc(s["u_ready"], 1)

            def scale_half(b, k, h):
                if known(b) or h:
                    act.wait_ge(s["uv_done"], b * 2 + h)
                act.activation(u_ps[:, :, :], f[:, k, :, H * h:H * h + H], ACT.Copy,
                               scale=dts[:, k:k + 1]).then_inc(s["u_ps_ready"], 1)

            scale_by_dt(0, 0)
            scale_half(0, 0, 0)
            act.dma_start(gamma[:, :], ln_gamma.partition_broadcast(P)).then_inc(s["small_in"], 16)
            act.dma_start(beta[:, :], ln_beta.partition_broadcast(P)).then_inc(s["small_in"], 16)
            act.wait_ge(s["edge_ready"], EDGE_OPS)
            act.activation(c_z[:, :, :].rearrange("p t d -> p (t d)"), c_z[:, :, :].rearrange("p t d -> p (t d)"), ACT.Copy, scale=0.25).then_inc(s["z_ready"], 1)
            act.wait_ge(s["sum_ready"], 1)
            act.activation(c_c[:, :, :].rearrange("p t d -> p (t d)"), c_c[:, :, :].rearrange("p t d -> p (t d)"), ACT.Copy, scale=-2.0).then_inc(s["c_ready"], 1)

            act.wait_ge(s["weights_t"], 1)
            act.activation(downT[:, :, :].rearrange("p c a -> p (c a)"), x_ps[0][:, :], ACT.Copy).then_inc(s["weights_ready"], 1)
            act.wait_ge(s["weights_t"], 2)
            act.activation(upT[:, :], x_ps[1][:, :], ACT.Copy).then_inc(s["weights_ready"], 1)
            act.wait_ge(s["vec_t"], 1)
            act.activation(vecT[:, :], y_ps[1][:, 0:P], ACT.Copy).then_inc(s["vec_ready"], 1)
            act.wait_ge(s["vec_ready"], 1)
            act.wait_ge(s["bias_ps"], 1)
            for c in range(CB):
                act.activation(biasT[:, c, :], y_ps[0][:, c * P:c * P + ROWS], ACT.Identity,
                               bias=vecT[:, V_UPB + c:V_UPB + c + 1]).then_inc(s["bias_ready"], 1)
            act.wait_ge(s["bias_ready"], CB)

            def comb_out(i, k, src):
                if known(i):
                    act.wait_ge(comb_stored[k], i * 16)
                act.activation(staged[:, k, DD:DD + CB], biasT[:, :, bass.ds(i * R + k, 1)].rearrange("p c a -> p (c a)"), ACT.Copy)
                act.activation(staged[:, k, 0:DD], src, ACT.Copy).then_inc(s["comb_sb_ready"], 1)

            def comb_row(i, k):
                act.wait_ge(s["comb_ps_ready"], i * R + (k + 1))
                comb_out(i, k, y_ps[k][:, :])

            for k in range(R):
                comb_row(0, k)
            scale_half(0, 0, 1)
            with act.Fori(1, E // R) as i:
                for k in range(R):
                    comb_row(i, k)
            for k in range(2):
                comb_out(E // R, k, upT[:, :])

            def statistics(q, n):
                if known(q):
                    act.wait_ge(s["squares_done"], q * 2)
                for j in range(2):
                    act.wait_ge(s["y_ready"], q * 2 + (j + 1))
                    act.activation(spent[:, j, :], y_ps[2 * (n % 2) + j][:, :], ACT.Identity,
                                   accum_out=total[:, n, j:j + 1]).then_inc(s["total_done"], 1)
                act.wait_ge(s["total_done"], q * 2 + 2)
                act.activation(neg_mean[:, n, :], total[:, n, :], ACT.Copy, scale=-1.0 / DD).then_inc(s["mean_done"], 1)
                act.wait_ge(s["mean_done"], q + 1)
                for j in range(2):
                    act.activation(spent[:, j, :], y_ps[2 * (n % 2) + j][:, :], ACT.Square, bias=neg_mean[:, n, j:j + 1],
                                   accum_out=squares[:, n, j:j + 1]).then_inc(s["squares_done"], 1)

            def body(b, k):
                last = isinstance(b, int) and b == NB - 1
                if known(b):
                    scale_half(b, k, 1)
                if known(b, 2):
                    statistics((b - 2) * 2 + 1, (2 * k + 1) % 4)
                if not last:
                    scale_by_dt(b + 1, 1 - k)
                if known(b):
                    act.wait_ge(s["h_ready"], b + 0)
                    act.wait_ge(s["xb_ready"], b * CB)
                for c in range(CB):
                    act.wait_ge(s["x_ready"], b * CB + (c + 1))
                    if isinstance(b, int) and b == 0 and c == 0:
                        act.wait_ge(s["ghosts_ready"], 1)
                    act.activation(xT[:, c, :], x_ps[(c + k) % 2][:, :], ACT.Relu).then_inc(s["x_taken"], 1)
                    if c == 1:
                        if known(b):
                            statistics((b - 1) * 2, (2 * (k - 1)) % 4)
                        if not last:
                            scale_half(b + 1, 1 - k, 0)
                act.wait_ge(comb_in[k], batch_combs(b, k))
                if known(b):
                    act.wait_ge(s["y_ready"], b * T)
                act.wait_ge(s["x_taken"], b * CB + CB)
                for c in range(CB):
                    act.activation(xbT[:, c, :], xT[:, c, :], ACT.Identity,
                                   bias=comb[:, k, DD + c:DD + c + 1]).then_inc(s["xb_ready"], 1)
                act.wait_ge(s["h_ready"], b + 1)
                act.activation(hT[:, :], x_ps[(CB + k) % 2][:, :], ACT.Gelu, bias=vecT[:, V_DOWNB:V_DOWNB + 1]).then_inc(s["hid_ready"], 1)

            all_batches(act, body)
            for q in range(2 * NB - 3, 2 * NB):
                statistics(q, q % 4)

        @block.tensor
        def _(pe):
            pe.wait_ge(s["wide_ready"], 1)
            pe.wait_ge(s["down_in"], 16)
            for c in range(CB):
                last = pe.transpose(x_ps[0][:, c * P:c * P + P], downN[:, c * P:c * P + P], ident)
            last.then_inc(s["weights_t"], 1)
            pe.wait_ge(s["up_in"], 16)
            for c in range(CB):
                last = pe.transpose(x_ps[1][:, c * P:c * P + P], upN[:, c * P:c * P + P], ident)
            last.then_inc(s["weights_t"], 1)
            pe.wait_ge(s["vec_sum"], 1)
            pe.transpose(y_ps[1][:, 0:P], vec_a, ident).then_inc(s["vec_t"], 1)
            pe.wait_ge(s["weights_ready"], 2)
            pe.wait_ge(s["vec_ready"], 1)
            for c in range(CB):
                last = pe.matmul(y_ps[0][:, c * P:c * P + ROWS], upT[:, c * P:c * P + P], vecT[:, 0:ROWS], start=True, stop=True)
            last.then_inc(s["bias_ps"], 1)

            def comb_row(i, k):
                pe.wait_ge(expert_in[k], i * 16 + 16)
                if known(i):
                    pe.wait_ge(s["comb_sb_ready"], i * R + (k + 1 - R))
                pe.matmul(y_ps[k][:, :], expert[:, k, :], upT[:, :], start=True, stop=True).then_inc(s["comb_ps_ready"], 1)

            pe.wait_ge(s["bias_ready"], CB)
            for k in range(R):
                comb_row(0, k)
            with pe.Fori(1, E // R) as i:
                for k in range(R):
                    comb_row(i, k)

            def stencil(b, k, h):
                if h == 0:
                    pe.wait_ge(f_in[k], batch_loads(b, k))
                pe.wait_ge(s["y_done"], b * 2 + (h + 1))
                pe.wait_ge(s["uv_done"], b * 2 + (h + 1))
                for c in (2 * h, 2 * h + 1):
                    if c >= 2:
                        pe.wait_ge(s["x_taken"], b * CB + (c - 1))
                    elif known(b):
                        pe.wait_ge(*((s["x_taken"], b * CB), (s["hid_ready"], b + 0))[c])
                    bank, cols, loc = x_ps[(c + k) % 2], slice(c * P, c * P + P), slice((c % 2) * P, (c % 2) * P + P)

                    def add(term, t_out, shift=None, start=False):
                        pe.matmul(bank[:, t_out * P:t_out * P + P], term, ident if shift is None else shift, start=start, stop=False,
                                  is_transpose=(shift is None), skip_group_check=True)

                    for t in range(T):
                        add(f[:, k, t, cols], t, start=(t == 0))
                    for t in range(T):
                        add(C[:, h, t, loc], t)
                    for t in range(T):
                        add(Yp[:, h, t, loc], t)
                    for t in range(T):
                        add(Ym[:, h, t, loc], t)
                    for t in range(T):
                        add(U[:, h, t, loc], (t - 1) % T, shift_up if t == 0 else None)
                    for t in range(T):
                        add(V[:, h, t, loc], (t + 1) % T, shift_down if t == T - 1 else None)
                    if isinstance(b, int) and b == 0 and c == 0:
                        pe.wait_ge(s["ghosts_ready"], 1)
                    pick = picks[:, :].rearrange("p (s b) -> p b s", b=NB)[:, bass.ds(b, 1), :].rearrange("p a s -> p (a s)")
                    pe.matmul(bank[:, 0:S:S - 1], ghosts[:, cols], pick, start=False, stop=True,
                              skip_group_check=True).then_inc(s["x_ready"], 1)

            def up(b, k, th):
                for t in (2 * th, 2 * th + 1):
                    if t == 0:
                        pe.wait_ge(s["hid_ready"], b + 1)
                        pe.wait_ge(comb_in[k], batch_combs(b, k))
                        pe.wait_ge(s["xb_ready"], b * CB + CB)
                    if known(b):
                        pe.wait_ge(s["g_done"], (b - 1) * T + (t + 1))
                    pe.matmul(y_ps[t][:, :], hT[:, t * P:t * P + P], comb[:, k, 0:DD], start=True, stop=False, skip_group_check=True)
                    for c in range(CB):
                        last = pe.matmul(y_ps[t][:, c * P:c * P + P], xbT[:, c, t * P:t * P + P], ident, start=False,
                                         stop=(c == CB - 1), is_transpose=True, skip_group_check=True)
                    last.then_inc(s["y_ready"], 1)

            def down(b, k):
                pe.wait_ge(s["x_taken"], b * CB + CB)
                for c in range(CB):
                    last = pe.matmul(x_ps[(CB + k) % 2][:, :], downT[:, c, :], xT[:, c, :], start=(c == 0), stop=(c == CB - 1))
                last.then_inc(s["h_ready"], 1)

            def body(b, k):
                for h in range(2):
                    stencil(b, k, h)
                    if known(b):
                        up(b - 1, 1 - k, h)
                down(b, k)

            all_batches(pe, body)
            for th in range(2):
                up(NB - 1, 1, th)

        @block.vector
        def _(dve):
            dve.memset(vec_a, 0.0).then_inc(s["zeroed"], 1)
            dve.memset(vec_b, 0.0).then_inc(s["zeroed"], 1)
            dve.memset(ghosts[:, :], 0.0).then_inc(s["zeroed"], 1)
            for r in range(4):
                p0, col = 2 * NB * (r // 2), slice(r % 2, r % 2 + 1)
                for w, first, last, scale in ((w_grad, GRAD[r], -GRAD[3 - r], 0.5), (w_grad2, GRAD2[r], GRAD2[3 - r], 0.5),
                                              (w_z, GRAD[r], -GRAD[3 - r], 0.25)):
                    dve.memset(w[p0:p0 + NB, col], first * scale)
                    dve.memset(w[p0 + NB:p0 + 2 * NB, col], last * scale).then_inc(s["border_step"], 1)
            n_border = [12]
            dve.wait_ge(s["wide_ready"], 1)
            dve.tensor_tensor(out=picks[:, :], in0=ident[:, 0:2 * NB], in1=ident[:, 2 * NB:4 * NB], op=ALU.add).then_inc(s["picks_ready"], 1)

            dve.wait_ge(s["ids_in"], 16)
            dve.tensor_scalar(idx_w[:, 0, :], idx_i[:, :], 0.0, float(E - 1), ALU.max, ALU.min).then_inc(s["idx_step"], 1)
            dve.tensor_scalar(idx_w[:, 1, :], idx_i[:, :], 0.0, float(KEEP0), ALU.is_lt, ALU.mult).then_inc(s["idx_step"], 1)
            dve.tensor_scalar(idx_w[:, 2, :], idx_i[:, :], float(E - 1), float(KEEPN - (E - 1)), ALU.is_gt, ALU.mult).then_inc(s["idx_step"], 1)
            dve.wait_ge(s["idx_step"], 3)
            dve.tensor_tensor(out=idx_w[:, 3, :], in0=idx_w[:, 0, :], in1=idx_w[:, 1, :], op=ALU.add).then_inc(s["idx_step"], 1)
            dve.wait_ge(s["idx_step"], 4)
            dve.tensor_tensor(out=rows[:, :], in0=idx_w[:, 3, :], in1=idx_w[:, 2, :], op=ALU.add).then_inc(s["rows_ready"], 1)

            dve.wait_ge(s["vecs_in"], 96)
            dve.tensor_tensor(out=vec_a, in0=vec_a, in1=vec_b, op=ALU.add).then_inc(s["vec_sum"], 1)

            def grids(plus, minus, half, n):
                hv = half.rearrange("p a b d -> p (a b) d")
                dve.wait_ge(s["half_ready"], n + 1)
                dve.scalar_tensor_tensor(out=plus[:, :, :], in0=minus[:, :, :], scalar=-0.5, in1=hv,
                                         op0=ALU.mult, op1=ALU.add).then_inc(s["coef_ready"], 1)
                dve.wait_ge(s["coef_ready"], 1 + 2 * n)
                dve.scalar_tensor_tensor(out=minus[:, :, :], in0=minus[:, :, :], scalar=0.5, in1=hv,
                                         op0=ALU.mult, op1=ALU.add).then_inc(s["coef_ready"], 1)

            dve.wait_ge(grid_in["A0"], 16)
            grids(c_xp, c_xm, halfX, 0)

            dve.wait_ge(grid_in["A1"], 16)
            dve.wait_ge(grid_in["B1"], 16)
            n_edge = 0
            for side in range(2):
                for j in range(4):
                    r = j if side == 0 else 3 - j
                    col = j if side == 0 else DD - 4 + j
                    sign = 1.0 if side == 0 else -1.0
                    w = c_yghost[:, side, :, j]
                    dve.tensor_scalar(w, c_yp[:, :, col], 0.5 * GRAD2[r], None, ALU.mult).then_inc(s["edge_ready"], 1)
                    n_edge += 1
                    if GRAD[r]:
                        dve.wait_ge(s["edge_ready"], n_edge)
                        dve.scalar_tensor_tensor(out=w, in0=c_ym[:, :, col], scalar=0.5 * sign * GRAD[r], in1=w,
                                                 op0=ALU.mult, op1=ALU.add).then_inc(s["edge_ready"], 1)
                        n_edge += 1
            dve.wait_ge(s["edge_ready"], n_edge)
            grids(c_yp, c_ym, halfY, 1)
            dve.wait_ge(grid_in["B2"], 16)
            for side in range(2):
                for j in range(3):
                    r = j if side == 0 else 2 - j
                    col = j if side == 0 else DD - 3 + j
                    sign = 1.0 if side == 0 else -1.0
                    dve.tensor_scalar(c_dedge[:, side, :, j], c_z[:, :, col], 0.25 * sign * EDGE[r], None, ALU.mult).then_inc(s["edge_ready"], 1)
                    n_edge += 1
            assert n_edge == EDGE_OPS
            dve.wait_ge(s["edge_ready"], EDGE_OPS)
            dve.wait_ge(s["coef_ready"], 4)
            dve.wait_ge(s["z_ready"], 1)

            def row_ghosts():
                def step(ins):
                    ins.then_inc(s["border_step"], 1)
                    n_border[0] += 1

                def settle():
                    dve.wait_ge(s["border_step"], n_border[0])

                dve.wait_ge(s["border_in"], 20 * 16)
                settle()
                step(dve.tensor_scalar(rf[:, :, :], rf[:, :, :], dt2[:, :], None, ALU.mult))
                settle()
                for r in range(2):
                    step(dve.scalar_tensor_tensor(out=rb2[:, r, :], in0=rb2[:, r, :], scalar=w_z[:, r:r + 1], in1=rf[:, r, :],
                                                  op0=ALU.mult, op1=ALU.mult))
                    step(dve.scalar_tensor_tensor(out=ra0[:, r, :], in0=ra0[:, r, :], scalar=w_grad[:, r:r + 1], in1=rf[:, r, :],
                                                  op0=ALU.mult, op1=ALU.mult))
                    step(dve.scalar_tensor_tensor(out=rb0[:, r, :], in0=rb0[:, r, :], scalar=w_grad2[:, r:r + 1], in1=rf[:, r, :],
                                                  op0=ALU.mult, op1=ALU.mult))
                settle()
                step(dve.tensor_tensor(out=ra0[:, :, :], in0=ra0[:, :, :], in1=rb0[:, :, :], op=ALU.add))
                step(dve.tensor_tensor(out=rb2[:, 0, :], in0=rb2[:, 0, :], in1=rb2[:, 1, :], op=ALU.add))
                settle()
                step(dve.tensor_tensor(out=ra0[:, 0, :], in0=ra0[:, 0, :], in1=ra0[:, 1, :], op=ALU.add))
                z, d = rb2[:, 0, :], rb2[:, 1, :]
                step(dve.tensor_tensor(out=d[:, 1:DD - 1], in0=z[:, 0:DD - 2], in1=z[:, 2:DD], op=ALU.subtract))
                for col, j1, j2, sign in ((0, 1, 2, 1.0), (DD - 1, DD - 2, DD - 3, -1.0)):
                    e = d[:, col:col + 1]
                    step(dve.tensor_scalar(e, z[:, col:col + 1], -sign * EDGE[0], None, ALU.mult))
                    settle()
                    for jj, wgt in ((j1, EDGE[1]), (j2, EDGE[2])):
                        step(dve.scalar_tensor_tensor(out=e, in0=z[:, jj:jj + 1], scalar=-sign * wgt, in1=e, op0=ALU.mult, op1=ALU.add))
                        settle()
                dve.wait_ge(s["zeroed"], 3)
                dve.tensor_tensor(out=ghosts[:, :], in0=ra0[:, 0, :], in1=d, op=ALU.add).then_inc(s["ghosts_ready"], 1)

            def row_terms(b, k, h):
                n = b * 2 + h
                J = slice(H * h, H * h + H)
                dve.wait_ge(s["u_ready"], b + 1)
                if known(b):
                    dve.wait_ge(s["x_ready"], (b - 1) * CB + (2 * h + 2))
                z0, z1 = (0, H + 1) if h == 0 else (H + 1, DD)
                dve.tensor_tensor(out=Z[:, :, z0:z1], in0=u[:, k, :, z0:z1], in1=c_z[:, :, z0:z1], op=ALU.mult).then_inc(s["z_done"], 1)


                dve.wait_ge(s["z_done"], n + 1)
                if h == 0:
                    dve.tensor_tensor(out=D[:, :, 1:H], in0=Z[:, :, 2:H + 1], in1=Z[:, :, 0:H - 1], op=ALU.subtract).then_inc(s["d_done"], 1)
                else:
                    dve.tensor_tensor(out=D[:, :, 0:H - 1], in0=Z[:, :, H + 1:DD], in1=Z[:, :, H - 1:DD - 2], op=ALU.subtract).then_inc(s["d_done"], 1)
                dve.wait_ge(s["edge_parts"], n + 1)
                ghost, edge = (Ym[:, h, :, 0:1], D[:, :, 0:1]) if h == 0 else (Yp[:, h, :, H - 1:H], D[:, :, H - 1:H])
                dve.tensor_reduce(ghost, yg_part[:, h, :, :], AX.X, ALU.add)
                dve.tensor_reduce(edge, de_part[:, h, :, :], AX.X, ALU.add).then_inc(s["edges_done"], 1)
                dve.wait_ge(s["u_ps_ready"], n + 1)
                if h == 1:
                    if isinstance(b, int) and b == 0:
                        dve.wait_ge(s["c_ready"], 1)
                    dve.tensor_tensor(out=C[:, h, :, :], in0=u_ps[:, :, :], in1=c_c[:, :, J], op=ALU.mult)
                dve.tensor_tensor(out=U[:, h, :, :], in0=u_ps[:, :, :], in1=c_xp[:, :, J], op=ALU.mult).then_inc(s["xp_done"], 1)
                dve.tensor_tensor(out=u_ps[:, :, :], in0=u_ps[:, :, :], in1=c_xm[:, :, J], op=ALU.mult).then_inc(s["xm_done"], 1)
                dve.wait_ge(s["d_done"], n + 1)
                dve.wait_ge(s["edges_done"], n + 1)
                dve.wait_ge(s["xp_done"], n + 1)
                dve.tensor_tensor(out=U[:, h, :, :], in0=U[:, h, :, :], in1=D[:, :, :], op=ALU.add)
                dve.wait_ge(s["xm_done"], n + 1)
                dve.tensor_tensor(out=V[:, h, :, :], in0=u_ps[:, :, :], in1=D[:, :, :], op=ALU.subtract).then_inc(s["uv_done"], 1)

            def centre(q, n):
                if isinstance(q, int) and q == 0:
                    dve.wait_ge(s["small_in"], 32)
                if known(q, 4):
                    dve.wait_ge(stored[n], (q - n) * 4)
                for j in range(2):
                    dve.wait_ge(s["squares_done"], q * 2 + (j + 1))
                    dve.scalar_tensor_tensor(out=g[:, n, j, :], in0=y_ps[2 * (n % 2) + j][:, :], scalar=neg_mean[:, n, j:j + 1],
                                             in1=gamma[:, :], op0=ALU.add, op1=ALU.mult).then_inc(s["g_done"], 1)

            def finish(q, n):
                dve.wait_ge(s["rstd_ready"], q + 1)
                dve.wait_ge(s["g_done"], q * 2 + 2)
                for j in range(2):
                    last = dve.scalar_tensor_tensor(out=g[:, n, j, :], in0=g[:, n, j, :], scalar=rstd[:, n, j:j + 1], in1=beta[:, :],
                                                    op0=ALU.mult, op1=ALU.add)
                last.then_inc(s["out_ready"], 1)

            def norm_slot(b, k, h):
                for back, what in ((4, centre), (5, finish)):
                    q = pair_of(b, k, h, back)
                    if q:
                        what(*q)

            def body(b, k):
                for h in range(2):
                    row_terms(b, k, h)
                    if isinstance(b, int) and (b, h) == (0, 0):
                        row_ghosts()
                    norm_slot(b, k, h)

            dve.wait_ge(s["weights_t"], 2)
            dve.wait_ge(s["vec_t"], 1)
            all_batches(dve, body)
            for m in range(5):
                q = 2 * NB - 4 + m
                if q < 2 * NB:
                    centre(q, q % 4)
                finish(q - 1, (q - 1) % 4)


_INS = ['x', 'condB_dt', 'itok_B_0_15', 'L0_cond_A_grid', 'L0_cond_B_grid', 'L1_cond_down_W', 'L1_cond_down_b',
        'L1_cond_up_W', 'L1_cond_up_b', 'L1_cond_expert_W', 'L1_cond_expert_b', 'L1_cond_domain_emb',
        'L1_cond_ln_gamma', 'L1_cond_ln_beta']


def kernel(**inputs):
    import numpy as _np
    import concourse.bacc as _bacc
    from concourse import mybir as _mybir
    from concourse.bass_utils import run_bass_kernel_spmd as _run

    nc = _bacc.Bacc("TRN2", target_bir_lowering=False, num_devices=1)
    arrays, args = {}, []
    for name in _INS:
        a = _np.ascontiguousarray(inputs[name])
        arrays[f"in_{name}_dram"] = a
        args.append(nc.dram_tensor(f"in_{name}_dram", a.shape, _mybir.dt.from_np(a.dtype), kind="ExternalInput").ap())
    args.append(nc.dram_tensor("out_0_dram", inputs["x"].shape, _mybir.dt.float32, kind="ExternalOutput").ap())
    stencil_adapter_kernel(nc, *args)
    r = _run(nc, [arrays], core_ids=[0])
    return r.results[0]["out_0_dram"]
```

```python
import concourse.bass as bass
from concourse import mybir
from contextlib import ExitStack


def stencil_adapter_kernel(nc, x, dt_b, expert_id, A_grid, B_grid, down_W, down_b, up_W, up_b,
                           expert_W, expert_b, domain_emb, ln_gamma, ln_beta, out):
    fp32, i32 = mybir.dt.float32, mybir.dt.int32
    ALU, ACT, AX = mybir.AluOpType, mybir.ActivationFunctionType, mybir.AxisListType

    NB, S, DD = x.shape
    A, E = down_b.shape[0], expert_b.shape[0]
    P = 128
    T = S // P
    CB = DD // P
    H = DD // 2
    R = 4
    EDGE_OPS = 20
    LEAD = 4
    EPS = 1e-5
    KEEP0, KEEPN, ROWS = E, E + 1, E + 2
    V_UPB, V_DOWNB = ROWS, ROWS + CB
    GRAD = (3.0, -3.0, 1.0, 0.0)
    GRAD2 = (4.0, -6.0, 4.0, -1.0)
    EDGE = (-3.0, 4.0, -1.0)

    x_v = x.rearrange("b (p t) d -> b p (t d)", t=T)
    out_v = out.rearrange("b (p t) d -> b p (t d)", t=T)
    grid_v = [g.rearrange("c (p t) d -> c p t d", t=T) for g in (A_grid, B_grid)]
    comb_dram = nc.dram_tensor("comb_dram", [ROWS, P, DD + CB], fp32, kind="Internal").ap()

    ctx = ExitStack()
    with ctx:
        def sb(name, shape, dt=fp32):
            return ctx.enter_context(nc.sbuf_tensor(name, shape, dt))

        def pb(name, shape):
            return ctx.enter_context(nc.psum_tensor(name, shape, fp32))

        def sem(name):
            return ctx.enter_context(nc.semaphore(name))

        c_xp, c_xm, c_yp, c_ym, c_c, c_z = (sb(n, [P, T, DD]) for n in ("c_xp", "c_xm", "c_yp", "c_ym", "c_c", "c_z"))
        c_yghost = sb("c_yghost", [P, 2, T, 4])
        c_dedge = sb("c_dedge", [P, 2, T, 3])
        wide = sb("wide", [P, P + 4])
        ident, shift_up, shift_down = wide[:, 2:P + 2], wide[:, 3:P + 3], wide[:, 1:P + 1]
        dts = sb("dts", [P, 2])
        gamma, beta = sb("gamma", [P, DD]), sb("beta", [P, DD])
        downT = sb("downT", [P, CB, A])
        upT = sb("upT", [A, DD])
        vecT = sb("vecT", [P, P])
        biasT = sb("biasT", [P, CB, ROWS])
        rows = sb("rows", [1, NB], i32)
        ghosts = sb("ghosts", [P, DD])
        picks = sb("picks", [P, 2 * NB])
        minus_half, one_over_d, eps = (sb(n, [P, 2]) for n in ("minus_half", "one_over_d", "eps"))
        one = sb("one", [P, 1])
        f = sb("f", [P, 2, T, DD])
        u = sb("u", [P, 2, T, DD])
        U, V, Yp, Ym, C = (sb(n, [P, 2, T, H]) for n in ("U", "V", "Yp", "Ym", "C"))
        Z = sb("Z", [P, T, DD])
        D = sb("D", [P, 2, T, H])
        W = sb("W", [P, T, H])
        yg_part = sb("yg_part", [P, 2, T, 4])
        de_part = sb("de_part", [P, 2, T, 3])
        xT = sb("xT", [P, CB, S])
        xbT = sb("xbT", [P, CB, S])
        hT = sb("hT", [A, S])
        comb = sb("comb", [P, 2, DD + CB])
        total = sb("total", [P, 4, 2])
        neg_mean = sb("neg_mean", [P, 4, 2])
        squares = sb("squares", [P, 4, 2])
        spent = sb("spent", [P, 2, DD])
        var = sb("var", [P, 4, 2])
        var_eps = sb("var_eps", [P, 4, 2])
        rstd = sb("rstd", [P, 4, 2])
        g = sb("g", [P, 4, 2, DD])
        rf, rb2 = xT[:, 2:4, :], xbT[:, 2:4, :]
        ra0, rb0 = xT[:, 0:2, :], xbT[:, 0:2, :]
        far_f, far_b2 = spent[0:2 * NB, 0, :], spent[0:2 * NB, 1, :]
        w_far = sb("w_far", [2 * NB, 1])
        w_grad, w_grad2, w_z = (sb(n, [P, 2]) for n in ("w_grad", "w_grad2", "w_z"))
        dt2 = sb("dt2", [P, 1])
        halfX, halfY = g[:, 0:2, :, :], g[:, 2:4, :, :]
        flat = lambda v: v.rearrange("p a b d -> p (a b d)")
        downN = U[:, 0, :, :].rearrange("p t h -> p (t h)")[:, 0:DD]
        upN = U[:, 1, :, :].rearrange("p t h -> p (t h)")[:, 0:DD]
        vec_a = V[:, 0, 0, 0:P]
        vec_b = V[:, 1, 0, 0:P]
        expert = halfX.rearrange("p n j d -> p (n j d)").rearrange("p (e a) -> p e a", e=E)
        staged = sb("staged", [P, R, DD + CB])
        idx_i = sb("idx_i", [1, NB], i32)
        idx_w = sb("idx_w", [1, 4, NB])

        x_ps = [pb(f"x_ps{n}", [P, S]) for n in range(2)]
        u_ps = pb("u_ps", [P, T, H])
        y_ps = [pb(f"y_ps{n}", [P, DD]) for n in range(T)]

        names = ("ends_zeroed w_ready expert_in small_in ids_in border_in vecs_in zeroed seeded wide_ready down_in up_in "
                 "half_ready sum_ready c_ready z_ready coef_ready edge_ready weights_t weights_ready vec_sum vec_t vec_ready bias_ps bias_ready "
                 "comb_ps_ready comb_sb_ready border_step ghosts_ready idx_step rows_ready "
                 "picks_ready u_ready u_ps_ready z_done d_done xp_done edge_parts edges_done xm_done uv_done y_done "
                 "x_ready x_taken xb_ready h_ready hid_ready y_ready total_done mean_done squares_done g_done var_done ve_done rstd_ready out_ready")
        s = {n: sem(n) for n in names.split()}
        grid_in = {n: sem(f"grid_in_{n}") for n in ("A0", "B0", "A1", "B1", "B2")}
        f_in = [sem(f"f_in{k}") for k in range(2)]
        comb_in = [sem(f"comb_in{k}") for k in range(2)]
        comb_stored = [sem(f"comb_stored{k}") for k in range(R)]
        stored = [sem(f"stored{n}") for n in range(4)]

        def known(n, least=1):
            return not isinstance(n, int) or n >= least

        def batch_loads(b, k):
            return (b - k) * 16 + 32

        def batch_combs(b, k):
            return (b - k) * 8 + 16

        def all_batches(eng, body):
            for b in range(LEAD):
                body(b, b % 2)
            with eng.Fori(LEAD // 2, NB // 2 - 1) as i:
                body(i * 2, 0)
                body(i * 2 + 1, 1)
            body(NB - 2, 0), body(NB - 1, 1)

        def pair_of(b, k, h, back):
            q = b * 2 + (h - back)
            return (q, (2 * k + h - back) % 4) if known(q, 0) else None

        block = ctx.enter_context(nc.Block())

        @block.sync
        def _(sp):
            sp.dma_start(downN, down_W).then_inc(s["down_in"], 16)
            sp.dma_start(upN.rearrange("p (c a) -> p c a", c=CB), up_W.rearrange("(c p) a -> p c a", p=P)).then_inc(s["up_in"], 16)
            sp.wait_ge(s["zeroed"], 2)
            sp.dma_start(vec_a[0:E, :], expert_b).then_inc(s["vecs_in"], 16)
            sp.dma_start(vec_b[0:E, :], domain_emb).then_inc(s["vecs_in"], 16)
            sp.dma_start(vec_b[KEEP0:KEEP0 + 1, :], domain_emb[0:1, :]).then_inc(s["vecs_in"], 16)
            sp.dma_start(vec_b[KEEPN:KEEPN + 1, :], domain_emb[E - 1:E, :]).then_inc(s["vecs_in"], 16)
            sp.dma_start(vec_b[V_UPB:V_UPB + CB, :], up_b.rearrange("(c p) -> c p", p=P)).then_inc(s["vecs_in"], 16)
            sp.dma_start(vec_b[V_DOWNB:V_DOWNB + 1, :], down_b.rearrange("(a p) -> a p", a=1)).then_inc(s["vecs_in"], 16)
            sp.dma_start(idx_i[:, :], expert_id.rearrange("(a b) -> a b", a=1)).then_inc(s["ids_in"], 16)
            sp.dma_start(c_xp[:, :, :], grid_v[1][0]).then_inc(grid_in["B0"], 16)

            sp.dma_start(c_xm[:, :, :], grid_v[0][0]).then_inc(grid_in["A0"], 16)
            sp.dma_start(c_yp[:, :, :], grid_v[1][1]).then_inc(grid_in["B1"], 16)
            sp.dma_start(c_ym[:, :, :], grid_v[0][1]).then_inc(grid_in["A1"], 16)
            sp.dma_start(f[:, 0, :, :], x_v[0]).then_inc(f_in[0], 16)
            sp.dma_start(dts[:, 0:1], dt_b[0:1].partition_broadcast(P)).then_inc(f_in[0], 16)
            sp.dma_start(c_z[:, :, :], grid_v[1][2]).then_inc(grid_in["B2"], 16)
            sp.wait_ge(s["coef_ready"], 2)
            sp.wait_ge(s["zeroed"], 3)
            sp.dma_start(c_xp[0:1, 0, :], ghosts[0:1, :]).then_inc(s["ends_zeroed"], 16)
            sp.dma_start(c_xm[P - 1:P, T - 1, :], ghosts[0:1, :]).then_inc(s["ends_zeroed"], 16)
            sp.wait_ge(s["sum_ready"], 1)
            sp.dma_start(expert, expert_W.rearrange("e p a -> p e a")).then_inc(s["expert_in"], 16)
            for m in range(2):
                for side in range(2):
                    r0 = 2 * m + (0, S - 4)[side]
                    p0 = 2 * NB * m + NB * side
                    p1 = p0 + NB
                    sp.dma_start(rf[p0:p1, :, :], x[:, r0:r0 + 2, :]).then_inc(s["border_in"], 16)
                    sp.dma_start(dt2[p0:p1, :], dt_b.rearrange("(b a) -> b a", a=1)).then_inc(s["border_in"], 16)
                    for dst, src in ((ra0[p0:p1], A_grid[0]), (rb0[p0:p1], B_grid[0]), (rb2[p0:p1, :, :], B_grid[2])):
                        sp.dma_start(dst, src[r0:r0 + 2, :].partition_broadcast(NB)).then_inc(s["border_in"], 16)
            for side in range(2):
                other, p0 = (S - 1, 0)[side], NB * side
                sp.dma_start(far_f[p0:p0 + NB, :], x[:, other, :]).then_inc(s["border_in"], 16)
                sp.dma_start(far_b2[p0:p0 + NB, :], B_grid[2][other].partition_broadcast(NB)).then_inc(s["border_in"], 16)
            sp.dma_start(f[:, 1, :, :], x_v[1]).then_inc(f_in[1], 16)
            sp.dma_start(dts[:, 1:2], dt_b[1:2].partition_broadcast(P)).then_inc(f_in[1], 16)

            def comb_store(i, k):
                sp.wait_ge(s["comb_sb_ready"], i * R + (k + 1))
                sp.dma_start(comb_dram[i * R + k], staged[:, k, :]).then_inc(comb_stored[k], 16)

            with sp.Fori(1, E // R) as i:
                for k in range(R):
                    comb_store(i - 1, k)
            for k in range(R):
                comb_store(E // R - 1, k)
            for k in range(2):
                comb_store(E // R, k)
            for k in range(R):
                sp.wait_ge(comb_stored[k], 16 * (E // R + (k < 2)))
            sp.wait_ge(s["rows_ready"], 1)

            def table_row(b):
                return sp.value_load(rows[0:1, bass.ds(b, 1)], min_val=0, max_val=ROWS - 1)

            def load_comb(e, k):
                sp.dma_start(comb[:, k, :], comb_dram[bass.ds(e, 1), :, :].rearrange("a p d -> p (a d)")).then_inc(comb_in[k], 16)

            load_comb(table_row(0), 0)

            def store_pair(q, slot):
                b2, th = q
                n = slot
                src = g[:, n, :, :].rearrange("p a d -> p (a d)")
                sp.dma_start(out_v[bass.ds(b2, 1), :, th * 2 * DD:(th + 1) * 2 * DD].rearrange("a p d -> p (a d)"),
                             src).then_inc(stored[n], 16)

            def body(b, k):
                next_row = None if isinstance(b, int) and b == NB - 1 else table_row(b + 1)
                following = b + 2 if isinstance(b, int) else sp.snap(b + 2)
                if known(b, 2):
                    for back, th in ((3, 1), (2, 0)):
                        if known(b, back):
                            sp.wait_ge(s["out_ready"], (b - back) * 2 + (th + 1))
                            store_pair((b - back, th), (2 * (k - back) + th) % 4)
                if not (isinstance(b, int) and b >= NB - 2):
                    sp.wait_ge(s["uv_done"], b * 2 + 2)
                    sp.wait_ge(s["y_done"], b * 2 + 2)
                    sp.dma_start(f[:, k, :, :], x_v[bass.ds(following, 1), :, :].rearrange("a p d -> p (a d)")
                                 ).then_inc(f_in[k], 16)
                    sp.dma_start(dts[:, k:k + 1], dt_b[bass.ds(following, 1)].partition_broadcast(P)).then_inc(f_in[k], 16)
                if next_row is not None:
                    if known(b):
                        sp.wait_ge(s["y_ready"], b * T)
                    load_comb(next_row, 1 - k)

            all_batches(sp, body)
            for q in range(2 * NB - 5, 2 * NB):
                sp.wait_ge(s["out_ready"], q + 1)
                store_pair((q // 2, q % 2), q % 4)
            for n in range(4):
                sp.wait_ge(stored[n], 16 * (NB // 2))

        @block.gpsimd
        def _(pool):
            pool.memset(wide[:, :], 0.0).then_inc(s["seeded"], 1)
            for tile, value in ((minus_half, -0.5), (one_over_d, 1.0 / DD), (eps, EPS), (one, 1.0)):
                pool.memset(tile[:, :], value).then_inc(s["seeded"], 1)
            pool.wait_ge(s["seeded"], 1)
            for n, first in enumerate((2, P + 2, 2 - P)):
                if n:
                    pool.wait_ge(s["wide_ready"], n)
                pool.affine_select(out=wide[:, :], in_=wide[:, :], compare_op=ALU.not_equal, fill=1.0,
                                   base=first, pattern=[[-1, P + 4]], channel_multiplier=1).then_inc(s["wide_ready"], 1)
            pool.wait_ge(s["half_ready"], 2)
            pool.tensor_tensor(out=c_c[:, :, :], in0=halfX.rearrange("p a b d -> p (a b) d"), in1=halfY.rearrange("p a b d -> p (a b) d"),
                               op=ALU.add).then_inc(s["sum_ready"], 1)
            pool.wait_ge(s["coef_ready"], 4)

            def products(b, k, h):
                J = slice(H * h, H * h + H)
                pool.wait_ge(s["u_ready"], b + 1)
                if known(b):
                    pool.wait_ge(s["x_ready"], (b - 1) * CB + (2 * h + 2))

                q = pair_of(b, k, h, 5)
                if q:
                    inverse_deviation(*q)
                e4, e3 = (slice(0, 4), slice(0, 3)) if h == 0 else (slice(DD - 4, DD), slice(DD - 3, DD))
                if known(b):
                    pool.wait_ge(s["edges_done"], (b - 1) * 2 + (h + 1))
                elif h == 0:
                    pool.wait_ge(s["edge_ready"], EDGE_OPS)
                pool.tensor_tensor(out=yg_part[:, h, :, :], in0=u[:, k, :, e4], in1=c_yghost[:, h, :, :], op=ALU.mult)
                pool.tensor_tensor(out=de_part[:, h, :, :], in0=u[:, k, :, e3], in1=c_dedge[:, h, :, :], op=ALU.mult).then_inc(s["edge_parts"], 1)
                a, lo, n = (1, 0, H - 1) if h == 0 else (0, H - 1, H)
                pool.tensor_tensor(out=Ym[:, h, :, a:a + n], in0=u[:, k, :, lo:lo + n], in1=c_ym[:, :, lo:lo + n], op=ALU.mult)
                lo, n = (1, H) if h == 0 else (H + 1, H - 1)
                last = pool.tensor_tensor(out=Yp[:, h, :, 0:n], in0=u[:, k, :, lo:lo + n], in1=c_yp[:, :, lo:lo + n], op=ALU.mult)
                if h == 0:
                    pool.wait_ge(s["w_ready"], b * 2 + 1)
                    last = pool.tensor_tensor(out=C[:, h, :, :], in0=f[:, k, :, J], in1=W[:, :, :], op=ALU.mult)
                last.then_inc(s["y_done"], 1)

            def inverse_deviation(q, n):
                pool.wait_ge(s["squares_done"], q * 2 + 2)
                pool.tensor_tensor(out=var[:, n, :], in0=squares[:, n, :], in1=one_over_d[:, :], op=ALU.mult).then_inc(s["var_done"], 1)
                pool.wait_ge(s["var_done"], q + 1)
                pool.tensor_tensor(out=var_eps[:, n, :], in0=var[:, n, :], in1=eps[:, :], op=ALU.add).then_inc(s["ve_done"], 1)
                pool.wait_ge(s["ve_done"], q + 1)
                pool.tensor_tensor(out=rstd[:, n, :], in0=var_eps[:, n, :], in1=minus_half[:, :], op=ALU.pow).then_inc(s["rstd_ready"], 1)

            def body(b, k):
                for h in range(2):
                    products(b, k, h)

            all_batches(pool, body)
            for q in range(2 * NB - 5, 2 * NB):
                inverse_deviation(q, q % 4)

        @block.scalar
        def _(act):
            act.wait_ge(s["weights_t"], 1)
            act.activation(downT[:, :, :].rearrange("p c a -> p (c a)"), x_ps[0][:, :], ACT.Copy).then_inc(s["weights_ready"], 1)
            act.wait_ge(s["weights_t"], 2)
            act.activation(upT[:, :], x_ps[1][:, :], ACT.Copy).then_inc(s["weights_ready"], 1)
            act.wait_ge(s["vec_t"], 1)
            act.activation(vecT[:, :], y_ps[1][:, 0:P], ACT.Copy).then_inc(s["vec_ready"], 1)
            act.wait_ge(s["vec_ready"], 1)
            act.wait_ge(s["bias_ps"], 1)
            for c in range(CB):
                act.activation(biasT[:, c, :], y_ps[0][:, c * P:c * P + ROWS], ACT.Identity,
                               bias=vecT[:, V_UPB + c:V_UPB + c + 1]).then_inc(s["bias_ready"], 1)
            act.wait_ge(s["bias_ready"], CB)

            act.wait_ge(grid_in["B0"], 16)
            act.activation(flat(halfX), c_xp[:, :, :].rearrange("p t d -> p (t d)"), ACT.Copy, scale=0.5).then_inc(s["half_ready"], 1)
            act.wait_ge(grid_in["B1"], 16)
            act.activation(flat(halfY), c_yp[:, :, :].rearrange("p t d -> p (t d)"), ACT.Copy, scale=0.5).then_inc(s["half_ready"], 1)

            def scale_by_dt(b, k):
                act.wait_ge(f_in[k], batch_loads(b, k))
                if known(b, 2):
                    act.wait_ge(s["uv_done"], (b - 1) * 2)
                    act.wait_ge(s["y_done"], (b - 1) * 2)
                act.activation(u[:, k, :, :].rearrange("p t d -> p (t d)"), f[:, k, :, :].rearrange("p t d -> p (t d)"),
                               ACT.Copy, scale=dts[:, k:k + 1]).then_inc(s["u_ready"], 1)

            def scale_half(b, k, h):
                if known(b) or h:
                    act.wait_ge(s["uv_done"], b * 2 + h)
                act.activation(u_ps[:, :, :], f[:, k, :, H * h:H * h + H], ACT.Copy,
                               scale=dts[:, k:k + 1]).then_inc(s["u_ps_ready"], 1)

            def centre_weights(b, k, h):
                if h:
                    act.wait_ge(s["y_done"], b * 2 + 1)
                elif known(b):
                    act.wait_ge(s["uv_done"], b * 2)
                act.activation(W[:, :, :], c_c[:, :, H * h:H * h + H], ACT.Identity, bias=one[:, :],
                               scale=dts[:, k:k + 1]).then_inc(s["w_ready"], 1)

            scale_by_dt(0, 0)
            scale_half(0, 0, 0)
            act.dma_start(gamma[:, :], ln_gamma.partition_broadcast(P)).then_inc(s["small_in"], 16)
            act.dma_start(beta[:, :], ln_beta.partition_broadcast(P)).then_inc(s["small_in"], 16)
            act.wait_ge(grid_in["B2"], 16)
            act.activation(c_z[:, :, :].rearrange("p t d -> p (t d)"), c_z[:, :, :].rearrange("p t d -> p (t d)"), ACT.Copy, scale=0.25).then_inc(s["z_ready"], 1)
            act.wait_ge(s["sum_ready"], 1)
            act.activation(c_c[:, :, :].rearrange("p t d -> p (t d)"), c_c[:, :, :].rearrange("p t d -> p (t d)"), ACT.Copy, scale=-2.0).then_inc(s["c_ready"], 1)
            act.wait_ge(s["c_ready"], 1)
            act.wait_ge(s["seeded"], 5)
            centre_weights(0, 0, 0)

            def comb_out(i, k, src):
                if known(i):
                    act.wait_ge(comb_stored[k], i * 16)
                act.activation(staged[:, k, DD:DD + CB], biasT[:, :, bass.ds(i * R + k, 1)].rearrange("p c a -> p (c a)"), ACT.Copy)
                act.activation(staged[:, k, 0:DD], src, ACT.Copy).then_inc(s["comb_sb_ready"], 1)

            def comb_row(i, k):
                act.wait_ge(s["comb_ps_ready"], i * R + (k + 1))
                comb_out(i, k, y_ps[k][:, :])

            for k in range(R):
                comb_row(0, k)
            scale_half(0, 0, 1)
            centre_weights(0, 0, 1)
            with act.Fori(1, E // R) as i:
                for k in range(R):
                    comb_row(i, k)
            for k in range(2):
                comb_out(E // R, k, upT[:, :])

            def statistics(q, n):
                if known(q):
                    act.wait_ge(s["squares_done"], q * 2)
                for j in range(2):
                    act.wait_ge(s["y_ready"], q * 2 + (j + 1))
                    act.activation(spent[:, j, :], y_ps[2 * (n % 2) + j][:, :], ACT.Identity,
                                   accum_out=total[:, n, j:j + 1]).then_inc(s["total_done"], 1)
                act.wait_ge(s["total_done"], q * 2 + 2)
                act.activation(neg_mean[:, n, :], total[:, n, :], ACT.Copy, scale=-1.0 / DD).then_inc(s["mean_done"], 1)
                act.wait_ge(s["mean_done"], q + 1)
                for j in range(2):
                    act.activation(spent[:, j, :], y_ps[2 * (n % 2) + j][:, :], ACT.Square, bias=neg_mean[:, n, j:j + 1],
                                   accum_out=squares[:, n, j:j + 1]).then_inc(s["squares_done"], 1)

            def body(b, k):
                last = isinstance(b, int) and b == NB - 1
                if known(b, 2):
                    statistics((b - 2) * 2 + 1, (2 * k + 1) % 4)
                if isinstance(b, int) and b == 0:
                    scale_by_dt(1, 1)
                    scale_half(1, 1, 0)
                    centre_weights(1, 1, 0)
                if known(b):
                    act.wait_ge(s["h_ready"], b + 0)
                    act.wait_ge(s["xb_ready"], b * CB)
                for c in range(CB):
                    act.wait_ge(s["x_ready"], b * CB + (c + 1))
                    if isinstance(b, int) and b == 0 and c == 0:
                        act.wait_ge(s["ghosts_ready"], 1)
                    act.activation(xT[:, c, :], x_ps[(c + k) % 2][:, :], ACT.Relu).then_inc(s["x_taken"], 1)
                    if c == 1 and known(b):
                        if not last:
                            scale_half(b + 1, 1 - k, 0)
                            centre_weights(b + 1, 1 - k, 0)
                        statistics((b - 1) * 2, (2 * (k - 1)) % 4)
                    if c == 2 and not (isinstance(b, int) and b >= NB - 2):
                        scale_by_dt(b + 2, k)
                if not last:
                    scale_half(b + 1, 1 - k, 1)
                    centre_weights(b + 1, 1 - k, 1)
                if last:
                    statistics((b - 1) * 2 + 1, (2 * k + 3) % 4)
                else:
                    act.wait_ge(comb_in[k], batch_combs(b, k))
                    if known(b):
                        act.wait_ge(s["y_ready"], b * T)
                    act.wait_ge(s["x_taken"], b * CB + CB)
                    for c in range(CB):
                        act.activation(xbT[:, c, :], xT[:, c, :], ACT.Identity,
                                       bias=comb[:, k, DD + c:DD + c + 1]).then_inc(s["xb_ready"], 1)
                act.wait_ge(s["h_ready"], b + 1)
                act.activation(hT[:, :], x_ps[(CB + k) % 2][:, :], ACT.Gelu, bias=vecT[:, V_DOWNB:V_DOWNB + 1]).then_inc(s["hid_ready"], 1)

            all_batches(act, body)
            for q in range(2 * NB - 2, 2 * NB):
                statistics(q, q % 4)

        @block.tensor
        def _(pe):
            pe.wait_ge(s["wide_ready"], 3)
            pe.wait_ge(s["down_in"], 16)
            for c in range(CB):
                last = pe.transpose(x_ps[0][:, c * P:c * P + P], downN[:, c * P:c * P + P], ident)
            last.then_inc(s["weights_t"], 1)
            pe.wait_ge(s["up_in"], 16)
            for c in range(CB):
                last = pe.transpose(x_ps[1][:, c * P:c * P + P], upN[:, c * P:c * P + P], ident)
            last.then_inc(s["weights_t"], 1)
            pe.wait_ge(s["vec_sum"], 1)
            pe.transpose(y_ps[1][:, 0:P], vec_a, ident).then_inc(s["vec_t"], 1)
            pe.wait_ge(s["weights_ready"], 2)
            pe.wait_ge(s["vec_ready"], 1)
            for c in range(CB):
                last = pe.matmul(y_ps[0][:, c * P:c * P + ROWS], upT[:, c * P:c * P + P], vecT[:, 0:ROWS], start=True, stop=True)
            last.then_inc(s["bias_ps"], 1)



            def comb_row(i, k):
                if isinstance(i, int) and (i, k) == (0, 0):
                    pe.wait_ge(s["expert_in"], 16)
                if known(i):
                    pe.wait_ge(s["comb_sb_ready"], i * R + (k + 1 - R))
                pe.matmul(y_ps[k][:, :], expert[:, i * R + k, :], upT[:, :], start=True, stop=True).then_inc(s["comb_ps_ready"], 1)

            pe.wait_ge(s["bias_ready"], CB)
            for k in range(R):
                comb_row(0, k)
            for i in range(1, E // R):
                for k in range(R):
                    comb_row(i, k)

            def stencil(b, k, h):
                pe.wait_ge(s["y_done"], b * 2 + (h + 1))
                pe.wait_ge(s["uv_done"], b * 2 + (h + 1))
                for c in (2 * h, 2 * h + 1):
                    if c >= 2:
                        pe.wait_ge(s["x_taken"], b * CB + (c - 1))
                    elif known(b):
                        pe.wait_ge(*((s["x_taken"], b * CB), (s["hid_ready"], b + 0))[c])
                    bank, cols, loc = x_ps[(c + k) % 2], slice(c * P, c * P + P), slice((c % 2) * P, (c % 2) * P + P)

                    def add(term, t_out, place=ident, start=False, stop=False):
                        return pe.matmul(bank[:, t_out * P:t_out * P + P], term, place, start=start, stop=stop,
                                         is_transpose=True, skip_group_check=True)

                    for t in range(T):
                        add(C[:, h, t, loc], t, start=(t == 0))
                    if isinstance(b, int) and b == 0 and c == 0:
                        pe.wait_ge(s["ghosts_ready"], 1)
                    pick = picks[:, :].rearrange("p (s b) -> p b s", b=NB)[:, bass.ds(b, 1), :].rearrange("p a s -> p (a s)")
                    pe.matmul(bank[:, 0:S:S - 1], ghosts[:, cols], pick, start=False, stop=False, skip_group_check=True)
                    for t in range(T):
                        add(Yp[:, h, t, loc], t)
                    for t in range(T):
                        add(Ym[:, h, t, loc], t)
                    for t in range(T):
                        add(U[:, h, t, loc], (t - 1) % T, shift_up if t == 0 else ident)
                    if c:
                        for t in range(T):
                            add(D[:, h, t, loc], (t - 1) % T, shift_up if t == 0 else ident)
                    for t in range(T):
                        last = add(V[:, h, t, loc], (t + 1) % T, shift_down if t == T - 1 else ident, stop=(t == T - 1))
                    last.then_inc(s["x_ready"], 1)

            def up(b, k, th):
                for t in (2 * th, 2 * th + 1):
                    if t == 0:
                        pe.wait_ge(s["hid_ready"], b + 1)
                        pe.wait_ge(comb_in[k], batch_combs(b, k))
                        pe.wait_ge(s["xb_ready"], b * CB + CB)
                    if known(b) and t == 2 * th:
                        pe.wait_ge(s["out_ready"], (b - 1) * 2 + (th + 1))
                    pe.matmul(y_ps[t][:, :], hT[:, t * P:t * P + P], comb[:, k, 0:DD], start=True, stop=False, skip_group_check=True)
                    for c in range(CB):
                        last = pe.matmul(y_ps[t][:, c * P:c * P + P], xbT[:, c, t * P:t * P + P], ident, start=False,
                                         stop=(c == CB - 1), is_transpose=True, skip_group_check=True)
                    last.then_inc(s["y_ready"], 1)

            def down(b, k):
                pe.wait_ge(s["x_taken"], b * CB + CB)
                for c in range(CB):
                    last = pe.matmul(x_ps[(CB + k) % 2][:, :], downT[:, c, :], xT[:, c, :], start=(c == 0), stop=(c == CB - 1))
                last.then_inc(s["h_ready"], 1)

            def body(b, k):
                for h in range(2):
                    stencil(b, k, h)
                    if known(b):
                        up(b - 1, 1 - k, h)
                down(b, k)

            all_batches(pe, body)
            for th in range(2):
                up(NB - 1, 1, th)

        @block.vector
        def _(dve):
            dve.memset(vec_a, 0.0).then_inc(s["zeroed"], 1)
            dve.memset(vec_b, 0.0).then_inc(s["zeroed"], 1)
            dve.memset(ghosts[:, :], 0.0).then_inc(s["zeroed"], 1)
            for r in range(4):
                p0, col = 2 * NB * (r // 2), slice(r % 2, r % 2 + 1)
                for w, first, last, scale in ((w_grad, GRAD[r], -GRAD[3 - r], 0.5), (w_grad2, GRAD2[r], GRAD2[3 - r], 0.5),
                                              (w_z, GRAD[r], -GRAD[3 - r], 0.25)):
                    dve.memset(w[p0:p0 + NB, col], first * scale)
                    dve.memset(w[p0 + NB:p0 + 2 * NB, col], last * scale).then_inc(s["border_step"], 1)
            dve.memset(w_far[0:NB, :], -0.25)
            dve.memset(w_far[NB:2 * NB, :], 0.25).then_inc(s["border_step"], 1)
            n_border = [13]
            dve.wait_ge(s["wide_ready"], 3)
            dve.tensor_tensor(out=picks[:, :], in0=ident[:, 0:2 * NB], in1=ident[:, 2 * NB:4 * NB], op=ALU.add).then_inc(s["picks_ready"], 1)

            dve.wait_ge(s["ids_in"], 16)
            dve.tensor_scalar(idx_w[:, 0, :], idx_i[:, :], 0.0, float(E - 1), ALU.max, ALU.min).then_inc(s["idx_step"], 1)
            dve.tensor_scalar(idx_w[:, 1, :], idx_i[:, :], 0.0, float(KEEP0), ALU.is_lt, ALU.mult).then_inc(s["idx_step"], 1)
            dve.tensor_scalar(idx_w[:, 2, :], idx_i[:, :], float(E - 1), float(KEEPN - (E - 1)), ALU.is_gt, ALU.mult).then_inc(s["idx_step"], 1)
            dve.wait_ge(s["idx_step"], 3)
            dve.tensor_tensor(out=idx_w[:, 3, :], in0=idx_w[:, 0, :], in1=idx_w[:, 1, :], op=ALU.add).then_inc(s["idx_step"], 1)
            dve.wait_ge(s["idx_step"], 4)
            dve.tensor_tensor(out=rows[:, :], in0=idx_w[:, 3, :], in1=idx_w[:, 2, :], op=ALU.add).then_inc(s["rows_ready"], 1)

            dve.wait_ge(s["vecs_in"], 96)
            dve.tensor_tensor(out=vec_a, in0=vec_a, in1=vec_b, op=ALU.add).then_inc(s["vec_sum"], 1)

            def grids(plus, minus, half, n):
                hv = half.rearrange("p a b d -> p (a b) d")
                dve.wait_ge(s["half_ready"], n + 1)
                dve.scalar_tensor_tensor(out=plus[:, :, :], in0=minus[:, :, :], scalar=-0.5, in1=hv,
                                         op0=ALU.mult, op1=ALU.add).then_inc(s["coef_ready"], 1)
                dve.wait_ge(s["coef_ready"], 1 + 2 * n)
                dve.scalar_tensor_tensor(out=minus[:, :, :], in0=minus[:, :, :], scalar=0.5, in1=hv,
                                         op0=ALU.mult, op1=ALU.add).then_inc(s["coef_ready"], 1)

            dve.wait_ge(grid_in["A0"], 16)
            grids(c_xp, c_xm, halfX, 0)

            dve.wait_ge(grid_in["A1"], 16)
            dve.wait_ge(grid_in["B1"], 16)
            n_edge = 0
            for side in range(2):
                for j in range(4):
                    r = j if side == 0 else 3 - j
                    col = j if side == 0 else DD - 4 + j
                    sign = 1.0 if side == 0 else -1.0
                    w = c_yghost[:, side, :, j]
                    dve.tensor_scalar(w, c_yp[:, :, col], 0.5 * GRAD2[r], None, ALU.mult).then_inc(s["edge_ready"], 1)
                    n_edge += 1
                    if GRAD[r]:
                        dve.wait_ge(s["edge_ready"], n_edge)
                        dve.scalar_tensor_tensor(out=w, in0=c_ym[:, :, col], scalar=0.5 * sign * GRAD[r], in1=w,
                                                 op0=ALU.mult, op1=ALU.add).then_inc(s["edge_ready"], 1)
                        n_edge += 1
            dve.wait_ge(s["edge_ready"], n_edge)
            grids(c_yp, c_ym, halfY, 1)
            dve.wait_ge(s["z_ready"], 1)
            for side in range(2):
                for j in range(3):
                    r = j if side == 0 else 2 - j
                    col = j if side == 0 else DD - 3 + j
                    sign = 1.0 if side == 0 else -1.0
                    dve.tensor_scalar(c_dedge[:, side, :, j], c_z[:, :, col], sign * EDGE[r], None, ALU.mult).then_inc(s["edge_ready"], 1)
                    n_edge += 1
            assert n_edge == EDGE_OPS
            dve.wait_ge(s["edge_ready"], EDGE_OPS)
            dve.wait_ge(s["coef_ready"], 4)

            def row_ghosts():
                def step(ins):
                    ins.then_inc(s["border_step"], 1)
                    n_border[0] += 1

                def settle():
                    dve.wait_ge(s["border_step"], n_border[0])

                dve.wait_ge(s["border_in"], 24 * 16)
                settle()
                step(dve.tensor_scalar(rf[:, :, :], rf[:, :, :], dt2[:, :], None, ALU.mult))
                step(dve.tensor_scalar(far_f, far_f, dt2[0:2 * NB, :], None, ALU.mult))
                settle()
                for r in range(2):
                    step(dve.scalar_tensor_tensor(out=rb2[:, r, :], in0=rb2[:, r, :], scalar=w_z[:, r:r + 1], in1=rf[:, r, :],
                                                  op0=ALU.mult, op1=ALU.mult))
                    step(dve.scalar_tensor_tensor(out=ra0[:, r, :], in0=ra0[:, r, :], scalar=w_grad[:, r:r + 1], in1=rf[:, r, :],
                                                  op0=ALU.mult, op1=ALU.mult))
                    step(dve.scalar_tensor_tensor(out=rb0[:, r, :], in0=rb0[:, r, :], scalar=w_grad2[:, r:r + 1], in1=rf[:, r, :],
                                                  op0=ALU.mult, op1=ALU.mult))
                step(dve.scalar_tensor_tensor(out=far_b2, in0=far_b2, scalar=w_far[:, :], in1=far_f, op0=ALU.mult, op1=ALU.mult))
                settle()
                step(dve.tensor_tensor(out=ra0[:, :, :], in0=ra0[:, :, :], in1=rb0[:, :, :], op=ALU.add))
                step(dve.tensor_tensor(out=rb2[:, 0, :], in0=rb2[:, 0, :], in1=rb2[:, 1, :], op=ALU.add))
                settle()
                step(dve.tensor_tensor(out=ra0[:, 0, :], in0=ra0[:, 0, :], in1=ra0[:, 1, :], op=ALU.add))
                step(dve.tensor_tensor(out=rb2[0:2 * NB, 0, :], in0=rb2[0:2 * NB, 0, :], in1=far_b2, op=ALU.add))
                settle()
                z, d = rb2[:, 0, :], rb2[:, 1, :]
                step(dve.tensor_tensor(out=d[:, 1:DD - 1], in0=z[:, 0:DD - 2], in1=z[:, 2:DD], op=ALU.subtract))
                for col, j1, j2, sign in ((0, 1, 2, 1.0), (DD - 1, DD - 2, DD - 3, -1.0)):
                    e = d[:, col:col + 1]
                    step(dve.tensor_scalar(e, z[:, col:col + 1], -sign * EDGE[0], None, ALU.mult))
                    settle()
                    for jj, wgt in ((j1, EDGE[1]), (j2, EDGE[2])):
                        step(dve.scalar_tensor_tensor(out=e, in0=z[:, jj:jj + 1], scalar=-sign * wgt, in1=e, op0=ALU.mult, op1=ALU.add))
                        settle()
                dve.wait_ge(s["ends_zeroed"], 32)
                dve.tensor_tensor(out=ghosts[:, :], in0=ra0[:, 0, :], in1=d, op=ALU.add).then_inc(s["ghosts_ready"], 1)

            def row_terms(b, k, h):
                n = b * 2 + h
                J = slice(H * h, H * h + H)
                dve.wait_ge(s["u_ready"], b + 1)
                if known(b):
                    dve.wait_ge(s["x_ready"], (b - 1) * CB + (2 * h + 2))
                if h == 0:
                    dve.tensor_tensor(out=Z[:, :, H:H + 1], in0=u[:, k, :, H:H + 1], in1=c_z[:, :, H:H + 1], op=ALU.mult)
                dve.wait_ge(s["u_ps_ready"], n + 1)
                dve.tensor_tensor(out=Z[:, :, J], in0=u_ps[:, :, :], in1=c_z[:, :, J], op=ALU.mult).then_inc(s["z_done"], 1)
                q = pair_of(b, k, h, 5)
                if q:
                    finish(*q)
                if isinstance(b, int) and n == 0:
                    dve.wait_ge(s["ends_zeroed"], 32)
                dve.tensor_tensor(out=U[:, h, :, :], in0=u_ps[:, :, :], in1=c_xp[:, :, J], op=ALU.mult).then_inc(s["xp_done"], 1)
                dve.wait_ge(s["z_done"], n + 1)
                if h == 0:
                    dve.tensor_tensor(out=D[:, h, :, 1:H], in0=Z[:, :, 2:H + 1], in1=Z[:, :, 0:H - 1], op=ALU.subtract).then_inc(s["d_done"], 1)
                else:
                    dve.tensor_tensor(out=D[:, h, :, 0:H - 1], in0=Z[:, :, H + 1:DD], in1=Z[:, :, H - 1:DD - 2], op=ALU.subtract).then_inc(s["d_done"], 1)
                dve.wait_ge(s["edge_parts"], n + 1)
                ghost, edge = (Ym[:, h, :, 0:1], D[:, h, :, 0:1]) if h == 0 else (Yp[:, h, :, H - 1:H], D[:, h, :, H - 1:H])
                dve.tensor_reduce(ghost, yg_part[:, h, :, :], AX.X, ALU.add)
                dve.tensor_reduce(edge, de_part[:, h, :, :], AX.X, ALU.add).then_inc(s["edges_done"], 1)
                dve.tensor_tensor(out=u_ps[:, :, :], in0=u_ps[:, :, :], in1=c_xm[:, :, J], op=ALU.mult).then_inc(s["xm_done"], 1)
                if h == 1:
                    dve.wait_ge(s["w_ready"], b * 2 + 2)
                    dve.tensor_tensor(out=C[:, h, :, :], in0=f[:, k, :, J], in1=W[:, :, :], op=ALU.mult)
                dve.wait_ge(s["d_done"], n + 1)
                dve.wait_ge(s["edges_done"], n + 1)
                if h == 0:
                    dve.wait_ge(s["xp_done"], n + 1)
                    dve.tensor_tensor(out=U[:, h, :, 0:P], in0=U[:, h, :, 0:P], in1=D[:, h, :, 0:P], op=ALU.add)
                dve.wait_ge(s["xm_done"], n + 1)
                dve.tensor_tensor(out=V[:, h, :, :], in0=u_ps[:, :, :], in1=D[:, h, :, :], op=ALU.subtract).then_inc(s["uv_done"], 1)

            def add_bias(b, k):
                dve.wait_ge(comb_in[k], batch_combs(b, k))
                dve.wait_ge(s["y_ready"], b * T)
                dve.wait_ge(s["x_taken"], b * CB + CB)
                for c in range(CB):
                    dve.tensor_scalar(xbT[:, c, :], xT[:, c, :], comb[:, k, DD + c:DD + c + 1], None,
                                      ALU.add).then_inc(s["xb_ready"], 1)

            def centre(q, n):
                if isinstance(q, int) and q == 0:
                    dve.wait_ge(s["small_in"], 32)
                for j in range(2):
                    y = y_ps[2 * (n % 2) + j][:, :]
                    dve.wait_ge(s["squares_done"], q * 2 + (j + 1))
                    dve.scalar_tensor_tensor(out=y, in0=y, scalar=neg_mean[:, n, j:j + 1],
                                             in1=gamma[:, :], op0=ALU.add, op1=ALU.mult).then_inc(s["g_done"], 1)

            def finish(q, n):
                if isinstance(q, int) and q == 0:
                    dve.wait_ge(s["comb_ps_ready"], E)
                if known(q, 4):
                    dve.wait_ge(stored[n], (q - n) * 4)
                dve.wait_ge(s["rstd_ready"], q + 1)
                dve.wait_ge(s["g_done"], q * 2 + 2)
                for j in range(2):
                    last = dve.scalar_tensor_tensor(out=g[:, n, j, :], in0=y_ps[2 * (n % 2) + j][:, :], scalar=rstd[:, n, j:j + 1], in1=beta[:, :],
                                                    op0=ALU.mult, op1=ALU.add)
                last.then_inc(s["out_ready"], 1)

            def norm_slot(b, k, h):
                q = pair_of(b, k, h, 4)
                if q:
                    centre(*q)

            def body(b, k):
                for h in range(2):
                    row_terms(b, k, h)
                    if isinstance(b, int) and (b, h) == (0, 0):
                        row_ghosts()
                    norm_slot(b, k, h)

            dve.wait_ge(s["weights_t"], 2)
            dve.wait_ge(s["vec_t"], 1)
            all_batches(dve, body)
            for m in range(5):
                q = 2 * NB - 4 + m
                finish(q - 1, (q - 1) % 4)
                if m == 1:
                    add_bias(NB - 1, 1)
                if q < 2 * NB:
                    centre(q, q % 4)


_INS = ['x', 'condB_dt', 'itok_B_0_15', 'L0_cond_A_grid', 'L0_cond_B_grid', 'L1_cond_down_W', 'L1_cond_down_b',
        'L1_cond_up_W', 'L1_cond_up_b', 'L1_cond_expert_W', 'L1_cond_expert_b', 'L1_cond_domain_emb',
        'L1_cond_ln_gamma', 'L1_cond_ln_beta']


def kernel(**inputs):
    import numpy as _np
    import concourse.bacc as _bacc
    from concourse import mybir as _mybir
    from concourse.bass_utils import run_bass_kernel_spmd as _run

    nc = _bacc.Bacc("TRN2", target_bir_lowering=False, num_devices=1)
    arrays, args = {}, []
    for name in _INS:
        a = _np.ascontiguousarray(inputs[name])
        arrays[f"in_{name}_dram"] = a
        args.append(nc.dram_tensor(f"in_{name}_dram", a.shape, _mybir.dt.from_np(a.dtype), kind="ExternalInput").ap())
    args.append(nc.dram_tensor("out_0_dram", inputs["x"].shape, _mybir.dt.float32, kind="ExternalOutput").ap())
    stencil_adapter_kernel(nc, *args)
    r = _run(nc, [arrays], core_ids=[0])
    return r.results[0]["out_0_dram"]
```
